# Optimizing a Trainium2 kernel written in Bass

```python
import numpy as np
import jax
import jax.numpy as jnp

def _softmax(x, axis=-1):
    return jax.nn.softmax(x, axis=axis)

def _gelu(x):
    return jax.nn.gelu(x, approximate=True)

def _silu(x):
    return jax.nn.silu(x)

def _sigmoid(x):
    return jax.nn.sigmoid(x)

def _layernorm(x, axis=-1, eps=1e-05):
    m = jnp.mean(x, axis=axis, keepdims=True)
    v = jnp.var(x, axis=axis, keepdims=True)
    return (x - m) / jnp.sqrt(v + eps)

def _scatter_add(tgt, idx, src, axis=0):
    return tgt.at[idx].add(src)

def _segment_sum(src, seg, n):
    return jax.ops.segment_sum(src, seg, n)
kernel_name = 'mk_recurrent_d1_jaxref_r8_870a1b'

def setup_inputs(seed: int=0):
    np.random.seed(seed)
    _w = jnp.asarray

    def _L0_attn_setup():
        import jax, jax.numpy as jnp
        import numpy as np
        N_HEADS = 16
        key = jax.random.key(seed)
        ks = jax.random.split(key, 5)
        B, S, D = (2, 256, 128)
        dk = D // N_HEADS
        std = float(np.sqrt(2.0 / (D + D)))
        x = jax.random.normal(ks[0], (B, S, D), dtype=jnp.float32)
        w_q = jax.random.normal(ks[1], (D, D), dtype=jnp.float32) * std
        w_k = jax.random.normal(ks[2], (dk, D), dtype=jnp.float32) * std
        w_v = jax.random.normal(ks[3], (dk, D), dtype=jnp.float32) * std
        w_out = jax.random.normal(ks[4], (D, D), dtype=jnp.float32) * std
        softmax_scale = jnp.ones((1,), dtype=jnp.float32) / jnp.sqrt(jnp.float32(dk))
        return {'x': x, 'w_q': w_q, 'w_k': w_k, 'w_v': w_v, 'w_out': w_out, 'softmax_scale': softmax_scale}
    _L0_attn_in = _L0_attn_setup()

    def _L0_ffn_setup():
        import jax, jax.numpy as jnp
        import numpy as np
        B, S, D = (1, 256, 128)
        I = 256
        E = 8
        K = 2
        LIMIT = 7.0
        ALPHA = 1.702
        EPS = 1e-05

        def _swiglu(h):
            x_glu = jnp.minimum(h[..., ::2], LIMIT)
            x_lin = jnp.clip(h[..., 1::2], -LIMIT, LIMIT)
            return x_glu * jax.nn.sigmoid(ALPHA * x_glu) * (x_lin + 1.0)

        def _moe(t, gate_w, gate_b, mlp1_w, mlp1_b, mlp2_w, mlp2_b):
            T = t.shape[0]
            logits = t @ gate_w + gate_b
            top_v, top_i = jax.lax.top_k(logits, K)
            probs = jax.nn.softmax(top_v, axis=-1)
            w = jnp.zeros((T, E), t.dtype).at[jnp.arange(T)[:, None], top_i].set(probs)

            def body(acc, ew):
                w1, b1, w2, b2, we = ew
                h = _swiglu(t @ w1 + b1)
                y = h @ w2 + b2
                return (acc + we[:, None] * y, None)
            acc0 = jnp.zeros((T, t.shape[1]), t.dtype)
            acc, _ = jax.lax.scan(body, acc0, (mlp1_w, mlp1_b, mlp2_w, mlp2_b, w.T))
            return acc
        key = jax.random.key(seed)
        ks = jax.random.split(key, 4)
        s = 0.02
        return {'x': jax.random.normal(ks[0], (B, S, D), jnp.float32), 'norm_scale': jnp.ones((D,), jnp.float32), 'gate_w': jax.random.normal(ks[1], (D, E), jnp.float32) * s, 'gate_b': jnp.zeros((E,), jnp.float32), 'mlp1_w': jax.random.normal(ks[2], (E, D, 2 * I), jnp.float32) * s, 'mlp1_b': jnp.zeros((E, 2 * I), jnp.float32), 'mlp2_w': jax.random.normal(ks[3], (E, I, D), jnp.float32) * s, 'mlp2_b': jnp.zeros((E, D), jnp.float32)}
    _L0_ffn_in = _L0_ffn_setup()
    _d = {'L0_attn_x': _L0_attn_in['x'], 'L0_attn_w_q': _L0_attn_in['w_q'], 'L0_attn_w_k': _L0_attn_in['w_k'], 'L0_attn_w_v': _L0_attn_in['w_v'], 'L0_attn_w_out': _L0_attn_in['w_out'], 'L0_attn_softmax_scale': _L0_attn_in['softmax_scale'], 'L0_ffn_norm_scale': _L0_ffn_in['norm_scale'], 'L0_ffn_gate_w': _L0_ffn_in['gate_w'], 'L0_ffn_gate_b': _L0_ffn_in['gate_b'], 'L0_ffn_mlp1_w': _L0_ffn_in['mlp1_w'], 'L0_ffn_mlp1_b': _L0_ffn_in['mlp1_b'], 'L0_ffn_mlp2_w': _L0_ffn_in['mlp2_w'], 'L0_ffn_mlp2_b': _L0_ffn_in['mlp2_b']}
    _x0 = _d['L0_attn_x']
    _d['L0_attn_x'] = jax.random.normal(jax.random.fold_in(jax.random.key(seed), 1), (16, 256, 128), dtype=_x0.dtype)
    del _x0
    return _d

def reference(L0_attn_x, L0_attn_w_q, L0_attn_w_k, L0_attn_w_v, L0_attn_w_out, L0_attn_softmax_scale, L0_ffn_norm_scale, L0_ffn_gate_w, L0_ffn_gate_b, L0_ffn_mlp1_w, L0_ffn_mlp1_b, L0_ffn_mlp2_w, L0_ffn_mlp2_b):

    def _L0_attn_ref(x, w_q, w_k, w_v, w_out, softmax_scale):
        import jax, jax.numpy as jnp
        import numpy as np
        N_HEADS = 16
        B, S, D = x.shape
        dk = D // N_HEADS
        q = (x @ w_q.T).reshape(B, S, N_HEADS, dk)
        k = x @ w_k.T
        v = x @ w_v.T
        scores = jnp.einsum('bshd,btd->bhst', q, k) * softmax_scale[0]
        attn = jax.nn.softmax(scores, axis=-1)
        out = jnp.einsum('bhst,btd->bshd', attn, v).reshape(B, S, D)
        return out @ w_out.T

    def _L0_ffn_ref(x, norm_scale, gate_w, gate_b, mlp1_w, mlp1_b, mlp2_w, mlp2_b):
        import jax, jax.numpy as jnp
        import numpy as np
        B, S, D = (1, 256, 128)
        I = 256
        E = 8
        K = 2
        LIMIT = 7.0
        ALPHA = 1.702
        EPS = 1e-05

        def _swiglu(h):
            x_glu = jnp.minimum(h[..., ::2], LIMIT)
            x_lin = jnp.clip(h[..., 1::2], -LIMIT, LIMIT)
            return x_glu * jax.nn.sigmoid(ALPHA * x_glu) * (x_lin + 1.0)

        def _moe(t, gate_w, gate_b, mlp1_w, mlp1_b, mlp2_w, mlp2_b):
            T = t.shape[0]
            logits = t @ gate_w + gate_b
            top_v, top_i = jax.lax.top_k(logits, K)
            probs = jax.nn.softmax(top_v, axis=-1)
            w = jnp.zeros((T, E), t.dtype).at[jnp.arange(T)[:, None], top_i].set(probs)

            def body(acc, ew):
                w1, b1, w2, b2, we = ew
                h = _swiglu(t @ w1 + b1)
                y = h @ w2 + b2
                return (acc + we[:, None] * y, None)
            acc0 = jnp.zeros((T, t.shape[1]), t.dtype)
            acc, _ = jax.lax.scan(body, acc0, (mlp1_w, mlp1_b, mlp2_w, mlp2_b, w.T))
            return acc
        Bx, Sx, Dx = x.shape
        ms = jnp.mean(x * x, axis=-1, keepdims=True)
        t = (x * jax.lax.rsqrt(ms + EPS) * norm_scale).reshape(Bx * Sx, Dx)
        y = _moe(t, gate_w, gate_b, mlp1_w, mlp1_b, mlp2_w, mlp2_b)
        return x + y.reshape(Bx, Sx, Dx)
    x = L0_attn_x
    xn = _layernorm(x, axis=-1)
    s = _L0_attn_ref(xn, L0_attn_w_q, L0_attn_w_k, L0_attn_w_v, L0_attn_w_out, L0_attn_softmax_scale)
    g = _silu(_L0_ffn_ref(xn, L0_ffn_norm_scale, L0_ffn_gate_w, L0_ffn_gate_b, L0_ffn_mlp1_w, L0_ffn_mlp1_b, L0_ffn_mlp2_w, L0_ffn_mlp2_b))
    x = x + s * g
    return x

_drawn_inputs = setup_inputs


def setup_inputs(seed=0):
    import zlib

    import numpy as np

    out = dict(_drawn_inputs(seed))
    spreads = {'L0_ffn_norm_scale': (1.0, 0.6),
     'L0_ffn_gate_b': (0.0, 0.8),
     'L0_ffn_mlp1_b': (0.0, 0.8),
     'L0_ffn_mlp2_b': (0.0, 0.8)}
    factors = {'L0_ffn_gate_w': 8.0, 'L0_ffn_mlp1_w': 8.0, 'L0_ffn_mlp2_w': 8.0}
    for name, (base, spread) in spreads.items():
        noise = np.random.default_rng([zlib.crc32(name.encode()), seed]).standard_normal(out[name].shape)
        drawn = base * np.exp(spread * noise) if base else spread * noise
        out[name] = jnp.asarray(drawn.astype(out[name].dtype))
    for name, factor in factors.items():
        out[name] = (out[name] * factor).astype(out[name].dtype)
    return out
```

```python
from contextlib import ExitStack

import numpy as np
import concourse.bass as bass
from concourse import mybir
from concourse.alu_op_type import AluOpType as ALU

ACT = mybir.ActivationFunctionType
F32 = mybir.dt.float32
BF16 = mybir.dt.bfloat16
I32 = mybir.dt.int32
AX = mybir.AxisListType.X

P = 128
B, S, D = 16, 256, 128
HEADS = 16
DK = D // HEADS
TOKENS = B * S
TILES = TOKENS // P
GROUPS = TILES // 4
E, INNER, TOPK = 8, 256, 2
LIMIT, ALPHA, EPS = 7.0, 1.702, 1e-5
UNITS = 2 * B
HU = HEADS // 2
UCOLS = HU * S
CH = 8
KROWS = 9 * DK
MROW = 96
SORTED = TOPK * TOKENS // P + E
PAIRS = SORTED // 2
ROW = D + 4
BIG = 3.0e38


def replicated(ap, times, at):
    dims = [list(d) for d in ap.ap]
    return bass.AP(ap.tensor, ap.offset, dims[:at] + [[0, times]] + dims[at:])


def await_ge(eng, semaphore, value, passed):
    eng.wait_ge(semaphore, value)
    if not isinstance(value, int):
        eng.sem_inc(passed, 1)


def build(nc, x, wq, w24, wout, nscale, gate_b, w1, b1, w2, b2, scale, out):
    ctx = ExitStack()
    with ctx:
        def sb(name, shape, dt=F32):
            return ctx.enter_context(nc.sbuf_tensor(name, shape, dt))

        def sem(name):
            return ctx.enter_context(nc.semaphore(name))

        q_dram = nc.dram_tensor("q_dram", [B, 3, P, S], BF16, kind="Internal").ap()
        bias_dram = nc.dram_tensor("bias_dram", [3, E * 2 * INNER + E * D], BF16, kind="Internal").ap()
        sorted_dram = nc.dram_tensor("sorted_dram", [SORTED * P, ROW], F32, kind="Internal").ap()
        y_dram = nc.dram_tensor("y_dram", [TOPK * TOKENS + SORTED * P, D], F32, kind="Internal").ap()

        x_all = sb("x_all", [P, TILES, D])
        xn_all = sb("xn_all", [P, TILES, D])
        s_all = sb("s_all", [P, TILES, D])
        w1_sb = sb("w1_sb", [P, E * 2 * INNER])
        w2_sb = sb("w2_sb", [P, E * 2 * D])
        bias_rows = sb("bias_rows", [3, E * 2 * INNER + E * D], BF16)
        wq_sb = sb("wq_sb", [P, D])
        wout_sb = sb("wout_sb", [P, D])
        w24_sb = sb("w24_sb", [P, 24])
        ns_col = sb("ns_col", [P, 1])
        ns_row = sb("ns_row", [P, D])
        gb_row = sb("gb_row", [P, E])
        sc_col = sb("sc_col", [P, 1])
        bias_in = sb("bias_in", [P, 40])
        bias_rest = sb("bias_rest", [P, 2, 40])
        bias_parts = sb("bias_parts", [P, 3, 40], BF16)
        ident = sb("ident", [P, P])
        ident_b = sb("ident_b", [P, P], BF16)
        before = sb("before", [P, P], BF16)
        ones_b = sb("ones_b", [P, P], BF16)
        ones_f = sb("ones_f", [P, P])
        rev8 = sb("rev8", [P, E])
        steps128 = sb("steps128", [P, TILES])
        tile_no = sb("tile_no", [P, SORTED])
        meta = sb("meta", [P, TILES, TOPK, 2])
        pad_row = sb("pad_row", [P, ROW])
        st6 = sb("st6", [P, TILES, 6])
        mv = sb("mv", [P, TILES, 2])
        lnb = sb("lnb", [P, 8, TILES])
        rstd, rms = lnb[:, 0, :], lnb[:, 1, :]
        xnT = sb("xnT", [P, 2, 512])
        q_all = sb("q_all", [P, TOKENS])
        q_parts = sb("q_parts", [P, 2, 3, 512], BF16)
        q_rest = sb("q_rest", [P, 2, 512])
        kvg = sb("kvg", [P, TILES, 24])
        k_p = sb("k_p", [P, 3, TILES, DK], BF16)
        k_stack = sb("k_stack", [P, TOKENS], BF16)
        v_all = sb("v_all", [P, TILES, 32])
        qs = sb("qs", [P, 4, UCOLS], BF16)
        k_max = sb("k_max", [P, 2, S], BF16)
        k_exp = sb("k_exp", [P, 2, S], BF16)
        v_use = sb("v_use", [P, 2, 2, 32])
        probs = sb("probs", [P, 2, CH, 512])
        maxes = sb("maxes", [P, 2, 2, HU])
        m_rest = sb("m_rest", [P, 2, 2, 2, HU])
        m_parts = sb("m_parts", [P, 2, 2, 3, HU], BF16)
        m_T = sb("m_T", [3 * HU, 2, S], BF16)
        o_T = sb("o_T", [P, 2, 512])
        inv_sum = sb("inv_sum", [P, 2, 4, 4])
        o_n = sb("o_n", [P, 2, D])
        o_nT = sb("o_nT", [P, S])
        rs = sb("rs", [P, 10, TILES])
        oh_b = sb("oh_b", [P, TILES * E], BF16)
        nt = sb("nt", [P, 6, 16])
        pos_i = sb("pos_i", [P, TILES, TOPK], I32)
        eid_f = sb("eid_f", [P, SORTED + 16])
        pow8 = sb("pow8", [P, 8])
        eid_p = sb("eid_p", [P, 10, 8])
        eid_s = sb("eid_s", [P, 2, 10])
        eid_i = sb("eid_i", [1, 2, 10], I32)
        pf = probs[:, :, :, :].rearrange("p a b c -> p (a b c)")
        rt = pf[:, 0:3072].rearrange("p (i c) -> p i c", i=12)
        scan = pf[:, 3072:3840].rearrange("p (i c) -> p i c", i=2)
        cmp_n = pf[:, 3840:4096].rearrange("p (e t) -> p e t", e=E)
        cmp_t = pf[:, 4096:4672].rearrange("p (t e) -> p t e", e=E)
        cmp_s = pf[:, 7232:7304]
        k_rest = pf[:, 4672:5184].rearrange("p (i t d) -> p i t d", i=2, d=DK)
        k_rows = pf[:, 5184:7232].bitcast(BF16).rearrange("p (t c) -> p t c", c=P)
        t_raw = sb("t_raw", [P, 2, D])
        r_col = sb("r_col", [P, 2, 1])
        pos_st = sb("pos_st", [P, 2, TOPK], I32)
        row_st = sb("row_st", [P, 2, TOPK, ROW])
        xs = sb("xs", [P, 4, 2, ROW])
        xT = pf[:, 0:512].rearrange("p (a c) -> p a c", a=2)
        glu = pf[:, 512:1536].rearrange("p (a c) -> p a c", a=2)
        lin = pf[:, 1536:2560].rearrange("p (a c) -> p a c", a=2)
        th = pf[:, 2560:3584].rearrange("p (a c) -> p a c", a=2)
        gt = pf[:, 3584:4608].rearrange("p (a c) -> p a c", a=2)
        hid = pf[:, 4608:5632].rearrange("p (a c) -> p a c", a=2)
        hT = pf[:, 5632:6144]
        ys = pf[:, 6144:7168].rearrange("p (a t c) -> p a t c", a=4, t=2)
        pad_at = sb("pad_at", [P, 4, 2])
        p_st = sb("p_st", [P, 4, 2])
        dest_i = sb("dest_i", [P, 4, 2], I32)
        yb = q_all[:, :].rearrange("p (a t c) -> p a t c", a=4, t=4)
        fb = [qs[:, i, :].bitcast(F32).rearrange("p (a c) -> p a c", a=2) for i in range(4)]

        ps = ctx.enter_context(nc.psum_tensor("ps", [P, 8, 512], F32))
        ex_bank = [ps[:, 0, :], ps[:, 1, :]]
        mx_bank = [ps[:, 2, :], ps[:, 3, :]]
        pv_bank = [ps[:, 4, :], ps[:, 5, :]]
        oT_bank = ps[:, 6, :]
        misc = ps[:, 7, :]

        names = """x_in w_in pad_in const_in stat var_ok std_ok ms_ok rms_ok xn_ok xT_ps xT_sb q_ps q_sb kv_ps kv_sb
            krow_ok kst_ps kst_sb v_ok bias_ok bias_w bias_r dve ones_in
            qpart q_w0 q_w1 qs_in0 qs_in1 qs_in2 qs_in3 km_in0 km_in1 ke_in0 ke_in1 v_in0 v_in1
            max_ps max_ok mpart mT_ps mT_sb m_in0 m_in1 exp_ps exp_ok pv_ok oT_sb oT_ps inv_ok on_ok onT_ps onT_sb
            s_ps s_ok oh_ok rank_ps e_ok e_exp route_ok prow pool_row scat0 scat1
            xs_in0 xs_in1 xs_in2 xs_in3 xsT_ps xsT_sb h_ps g_ok l_ok th_ok gt_ok hid_ok hT_ps hT_sb y_ps y_ok dest_ok p_ok y_out0 y_out1 y_out2 y_out3
            yb_in0 yb_in1 yb_in2 yb_in3 f_ok fth_ok o_ok out_done pool_passed sp_passed pe_passed""".split()
        m = {n: sem(n) for n in names}
        q_w = [m["q_w0"], m["q_w1"]]
        qs_in = [m[f"qs_in{i}"] for i in range(4)]
        km_in, ke_in, v_in = ([m[f"{n}_in{i}"] for i in range(2)] for n in ("km", "ke", "v"))
        m_in = [m["m_in0"], m["m_in1"]]
        xs_in = [m[f"xs_in{i}"] for i in range(4)]
        yb_in = [m[f"yb_in{i}"] for i in range(4)]
        scat = [m["scat0"], m["scat1"]]
        y_out = [m[f"y_out{i}"] for i in range(4)]
        N_W = 11

        def attention(eng, step):
            for u in range(-2, 4):
                step(u, u)
            with eng.Fori(1, UNITS // 4 - 1) as it:
                for r in range(4):
                    step(4 * it + r, 4 + r)
            for u in range(UNITS - 4, UNITS + 3):
                step(u, u)

        def experts(eng, step):
            for q in range(-1, 8):
                step(q, q)
            with eng.Fori(2, PAIRS // 4 - 1) as it:
                for r in range(4):
                    step(4 * it + r, 8 + r)
            for q in range(PAIRS - 4, PAIRS + 2):
                step(q, q)

        block = ctx.enter_context(nc.Block())

        @block.sync
        def _(sp):
            xv = x.rearrange("(t p) d -> p t d", p=P)
            for g in range(GROUPS):
                sp.dma_start(x_all[:, 4 * g:4 * g + 4, :], xv[:, 4 * g:4 * g + 4, :]).then_inc(m["x_in"], 16)
            for dst, src in (
                (wq_sb[:, :], wq), (w24_sb[:, :], w24), (wout_sb[:, :], wout),
                (ns_col[:, :], nscale.rearrange("(d a) -> d a", a=1)),
                (ns_row[:, :], nscale.rearrange("(a d) -> a d", a=1).to_broadcast([P, D])),
                (gb_row[:, :], gate_b.rearrange("(a d) -> a d", a=1).to_broadcast([P, E])),
                (sc_col[:, :], scale.rearrange("(a d) -> a d", a=1).to_broadcast([P, 1])),
                (bias_in[:, 0:32], b1.rearrange("(p c) -> p c", p=P)),
                (bias_in[:, 32:40], b2.rearrange("(p c) -> p c", p=P)),
            ):
                sp.dma_start(dst, src).then_inc(m["w_in"], 16)
            sp.dma_start(w1_sb[:, :], w1).then_inc(m["w_in"], 16)
            sp.dma_start(w2_sb[:, :], w2).then_inc(m["w_in"], 16)
            await_ge(sp, m["const_in"], 1, m["sp_passed"])
            sp.dma_start(sorted_dram.rearrange("(t p) c -> p t c", p=P),
                         replicated(pad_row[:, :], SORTED, 1)).then_inc(m["pad_in"], 16)
            await_ge(sp, m["bias_ok"], 1, m["sp_passed"])
            n1 = E * 2 * INNER
            sp.dma_start(bias_dram[:, 0:n1].rearrange("i (p c) -> p i c", p=P),
                         bias_parts[:, :, 0:32]).then_inc(m["bias_w"], 16)
            sp.dma_start(bias_dram[:, n1:].rearrange("i (p c) -> p i c", p=P),
                         bias_parts[:, :, 32:40]).then_inc(m["bias_w"], 16)
            await_ge(sp, m["bias_w"], 32, m["sp_passed"])
            sp.dma_start(bias_rows[:, :], bias_dram).then_inc(m["bias_r"], 16)

            def write_q(g, r):
                await_ge(sp, m["qpart"], 4 * g + 4, m["sp_passed"])
                for b in range(2):
                    sp.dma_start(q_dram[bass.ds(2 * g + b, 1)].rearrange("a i p s -> p (a i) s"),
                                 q_parts[:, r, :, b * S:(b + 1) * S]).then_inc(q_w[r], 16)

            def load_q(u, n, g, gn):
                await_ge(sp, q_w[gn % 2], 32 * (g // 2) + 32, m["sp_passed"])
                if n >= 4:
                    await_ge(sp, m["exp_ps"], CH * (u - 3), m["sp_passed"])
                src = q_dram[bass.ds(2 * g + (n % 4) // 2, 1)].rearrange("a i (d h) s -> (a i d) (h s)", d=DK)
                src = src[:, (n % 2) * UCOLS:(n % 2 + 1) * UCOLS]
                sp.dma_start(qs[0:KROWS, n % 4, :], replicated(src, 3, 0)).then_inc(qs_in[n % 4], 16)

            def load_k(dst, b, s):
                sp.dma_start(dst, k_stack[:, bass.ds(b * S, S)]).then_inc(s, 16)

            def load_v(b, n):
                sp.dma_start(v_use[:, n % 2, :, :], v_all[:, bass.ds(2 * b, 2), :]).then_inc(v_in[n % 2], 16)

            await_ge(sp, m["ones_in"], 1, m["sp_passed"])
            write_q(0, 0)
            for u in range(3):
                load_q(u, u, 0, 0)
            await_ge(sp, m["kst_sb"], 4, m["sp_passed"])
            await_ge(sp, m["v_ok"], 2, m["sp_passed"])
            load_k(k_max[:, 0, :], 0, km_in[0])
            load_k(k_max[:, 1, :], 1, km_in[1])
            load_k(k_exp[:, 0, :], 0, ke_in[0])
            load_v(0, 0)

            def turn(u, n):
                if n >= 0:
                    loads(u, n)
                if -1 <= n <= UNITS - 2:
                    await_ge(sp, m["mT_sb"], u + 2, m["sp_passed"])
                    sp.dma_start(qs[MROW:MROW + 3, (n + 1) % 4, :], m_T[:, (n + 1) % 2, :]
                                 ).then_inc(m_in[(n + 1) % 2], 16)

            def loads(u, n):
                if n % 4 == 0 and n + 4 < UNITS:
                    write_q(u // 4 + 1, (n // 4 + 1) % 2)
                if n + 3 < UNITS:
                    load_q(u + 3, n + 3, (u - n % 4) // 4 + (n % 4 + 3) // 4, n // 4 + (n % 4 + 3) // 4)
                if n % 2 == 0 and n // 2 + 2 < B:
                    await_ge(sp, m["max_ps"], CH * (u + 2), m["sp_passed"])
                    load_k(k_max[:, (n // 2) % 2, :], (u - n % 2) // 2 + 2, km_in[(n // 2) % 2])
                if n % 2 == 0 and n // 2 + 1 < B:
                    if n >= 2:
                        await_ge(sp, m["exp_ps"], CH * u, m["sp_passed"])
                    load_k(k_exp[:, (n // 2 + 1) % 2, :], (u - n % 2) // 2 + 1, ke_in[(n // 2 + 1) % 2])
                if n % 2 == 1 and n // 2 + 1 < B:
                    if n >= 3:
                        await_ge(sp, m["pv_ok"], u - 1, m["sp_passed"])
                    load_v((u - 1) // 2 + 1, n // 2 + 1)

            for u in range(-1, 8):
                turn(u, u)
            with sp.Fori(1, 3) as it:
                for r in range(8):
                    turn(8 * it + r, 8 + r)
            for u in range(24, UNITS):
                turn(u, u)

            await_ge(sp, scat[0], 8 * TOPK * TILES, m["sp_passed"])

            await_ge(sp, scat[1], 8 * TOPK * TILES, m["sp_passed"])

            def load_sorted(q, n):
                if n >= 4:
                    await_ge(sp, m["xsT_ps"], q - 3, m["sp_passed"])
                    await_ge(sp, m["p_ok"], q - 3, m["sp_passed"])
                    await_ge(sp, m["dest_ok"], 3 * (q - 3), m["sp_passed"])
                sp.dma_start(xs[:, n % 4, :, :],
                             sorted_dram[bass.ds(q * 2 * P, 2 * P), :].rearrange("(t p) c -> p t c", p=P)
                             ).then_inc(xs_in[n % 4], 16)

            for q in range(4):
                load_sorted(q, q)
            with sp.Fori(1, PAIRS // 4) as it:
                for r in range(4):
                    load_sorted(4 * it + r, 4 + r)

            for r in range(4):
                await_ge(sp, y_out[r], 4 * SORTED, m["sp_passed"])
            yv = y_dram[0:TOPK * TOKENS, :].rearrange("(t p k) d -> p t (k d)", p=P, k=TOPK)
            ov = out.rearrange("(t p) d -> p t d", p=P)
            for g in range(4):
                sp.dma_start(yb[:, g, :, :], yv[:, 4 * g:4 * g + 4, :]).then_inc(yb_in[g], 16)
            for g in range(GROUPS):
                await_ge(sp, m["o_ok"], g + 1, m["sp_passed"])
                sp.dma_start(ov[:, 4 * g:4 * g + 4, :], x_all[:, 4 * g:4 * g + 4, :]).then_inc(m["out_done"], 16)
                if g + 4 < GROUPS:
                    sp.dma_start(yb[:, g, :, :], yv[:, 4 * g + 16:4 * g + 20, :]).then_inc(yb_in[g], 16)
            await_ge(sp, m["out_done"], 16 * GROUPS, m["sp_passed"])

        @block.gpsimd
        def _(pool):
            gp = nc.gpsimd
            count = [0]

            def link(ins):
                count[0] += 1
                ins.then_inc(m["prow"], 1)
                await_ge(pool, m["prow"], count[0], m["pool_passed"])

            link(gp.memset(pad_row[:, :], 0.0))
            link(gp.memset(pad_row[:, D + 2:D + 3], float(P)))
            gp.iota(pad_row[:, D:D + 1], pattern=[[0, 1]], base=TOPK * TOKENS, channel_multiplier=1,
                    allow_small_or_imprecise_dtypes=True).then_inc(m["const_in"], 1)
            link(gp.memset(ones_f[:, :], 1.0))
            gp.memset(ones_b[:, :], 1.0)
            link(gp.affine_select(out=ident[:, :], in_=ones_f[:, :], compare_op=ALU.is_equal, fill=0.0, base=0,
                                  pattern=[[-1, P]], channel_multiplier=1))
            gp.tensor_copy(ident_b[:, :], ident[:, :])
            gp.affine_select(out=before[:, :], in_=ones_f[:, :], compare_op=ALU.is_gt, fill=0.0, base=0,
                             pattern=[[1, P]], channel_multiplier=-1)
            gp.iota(rev8[:, :], pattern=[[-1, E]], base=E, channel_multiplier=0, allow_small_or_imprecise_dtypes=True)
            gp.iota(steps128[:, :], pattern=[[P, TILES]], base=0, channel_multiplier=0,
                    allow_small_or_imprecise_dtypes=True)
            gp.iota(tile_no[:, :], pattern=[[1, SORTED]], base=0, channel_multiplier=0,
                    allow_small_or_imprecise_dtypes=True)
            gp.iota(meta[:, :, :, 0], pattern=[[TOPK * P, TILES], [1, TOPK]], base=0, channel_multiplier=TOPK,
                    allow_small_or_imprecise_dtypes=True)
            gp.memset(row_st[:, :, :, :], 0.0)
            gp.memset(eid_f[:, :], 0.0)
            for i in range(8):
                gp.memset(pow8[:, i:i + 1], float(8 ** i))
            gp.memset(scan[:, :, :], 0.0)
            gp.memset(k_rows[:, :, KROWS:P], 0.0).then_inc(m["const_in"], 1)
            await_ge(pool, m["const_in"], 2, m["pool_passed"])
            gp.memset(k_rows[:, :, MROW:MROW + 3], 1.0)
            link(gp.memset(v_all[:, :, :], 0.0))
            gp.memset(v_all[:, :, DK:DK + 1], 1.0).then_inc(m["const_in"], 1)
            gp.memset(qs[:, :, :].bitcast(F32), 0.0).then_inc(m["ones_in"], 1)

            def split_q(g, n):
                r = n % 2
                qv = q_all[:, bass.ds(g * 512, 512)]
                await_ge(pool, m["q_sb"], g + 1, m["pool_passed"])
                if n >= 2:
                    await_ge(pool, q_w[r], 32 * ((g - r) // 2), m["pool_passed"])
                gp.tensor_copy(q_parts[:, r, 0, :], qv).then_inc(m["qpart"], 1)
                await_ge(pool, m["qpart"], 4 * g + 1, m["pool_passed"])
                gp.tensor_tensor(q_rest[:, r, :], qv, q_parts[:, r, 0, :], ALU.subtract).then_inc(m["qpart"], 1)
                await_ge(pool, m["qpart"], 4 * g + 2, m["pool_passed"])
                gp.tensor_copy(q_parts[:, r, 1, :], q_rest[:, r, :]).then_inc(m["qpart"], 1)
                await_ge(pool, m["qpart"], 4 * g + 3, m["pool_passed"])
                gp.tensor_tensor(q_parts[:, r, 2, :], q_rest[:, r, :], q_parts[:, r, 1, :],
                                 ALU.subtract).then_inc(m["qpart"], 1)

            PER = 6

            def scatter(t, n):
                r = n % 2
                done = PER * t
                if n >= 2:
                    await_ge(pool, scat[r], 32 * ((t - r) // 2), m["pool_passed"])
                gp.tensor_copy(r_col[:, r, :], lnb[:, 1, bass.ds(t, 1)]).then_inc(m["pool_row"], 1)
                gp.tensor_tensor(t_raw[:, r, :], xn_all[:, bass.ds(t, 1), :].rearrange("p a d -> p (a d)"),
                                 ns_row[:, :], ALU.mult).then_inc(m["pool_row"], 1)
                gp.tensor_copy(pos_st[:, r, :], pos_i[:, bass.ds(t, 1), :].rearrange("p a k -> p (a k)")
                               ).then_inc(m["pool_row"], 1)
                gp.tensor_copy(row_st[:, r, :, D:D + 2], meta[:, bass.ds(t, 1), :, :].rearrange("p a k c -> p (a k) c")
                               ).then_inc(m["pool_row"], 1)
                await_ge(pool, m["pool_row"], done + 4, m["pool_passed"])
                for k in range(TOPK):
                    gp.tensor_scalar(row_st[:, r, k, 0:D], t_raw[:, r, :], r_col[:, r, :], 1.0,
                                     ALU.mult, ALU.mult).then_inc(m["pool_row"], 1)
                await_ge(pool, m["pool_row"], done + PER, m["pool_passed"])
                for k in range(TOPK):
                    gp.indirect_dma_start(out=sorted_dram, out_offset=bass.IndirectOffsetOnAxis(ap=pos_st[:, r, k:k + 1], axis=0),
                                          in_=row_st[:, r, k, :], in_offset=None).then_inc(scat[r], 16)

            split_q(0, 0)
            split_q(1, 1)
            await_ge(pool, m["route_ok"], 1, m["pool_passed"])
            await_ge(pool, m["pad_in"], 16, m["pool_passed"])
            await_ge(pool, m["w_in"], 16 * N_W, m["pool_passed"])
            for t in range(4):
                scatter(t, t)
            with pool.Fori(1, GROUPS // 2) as it:
                for h in range(2):
                    split_q(2 * it + h, 2 + h)
                    for r in range(4):
                        scatter(8 * it + 4 * h + r - 4, 4 + r)
            for t in range(TILES - 4, TILES):
                scatter(t, t)

            def prepare(q, n):
                r = n % 4
                await_ge(pool, xs_in[r], 16 * ((q - r) // 4) + 16, m["pool_passed"])
                if n >= 4:
                    await_ge(pool, y_out[r], 32 * ((q - r) // 4), m["pool_passed"])
                gp.tensor_tensor(pad_at[:, r, :], xs[:, r, :, D + 2], tile_no[:, bass.ds(2 * q, 2)], ALU.mult
                                 ).then_inc(m["dest_ok"], 1)
                await_ge(pool, m["dest_ok"], 3 * q + 1, m["pool_passed"])
                gp.tensor_tensor(pad_at[:, r, :], xs[:, r, :, D], pad_at[:, r, :], ALU.add).then_inc(m["dest_ok"], 1)
                await_ge(pool, m["dest_ok"], 3 * q + 2, m["pool_passed"])
                if n >= 4:
                    await_ge(pool, m["y_ok"], 2 * (q - 3), m["pool_passed"])
                gp.tensor_copy(p_st[:, r, :], xs[:, r, :, D + 1]).then_inc(m["p_ok"], 1)
                gp.tensor_copy(dest_i[:, r, :], pad_at[:, r, :]).then_inc(m["dest_ok"], 1)
                await_ge(pool, m["dest_ok"], 3 * q + 3, m["pool_passed"])

            def send(q, n):
                r = n % 4
                await_ge(pool, m["y_ok"], 2 * q + 2, m["pool_passed"])
                for t in range(2):
                    gp.indirect_dma_start(out=y_dram, out_offset=bass.IndirectOffsetOnAxis(ap=dest_i[:, r, t:t + 1], axis=0),
                                          in_=ys[:, r, t, :], in_offset=None).then_inc(y_out[r], 16)

            for q in range(3):
                prepare(q, q)
            prepare(3, 3)
            send(0, 0)
            with pool.Fori(1, PAIRS // 4) as it:
                for r in range(4):
                    prepare(4 * it + r, 4 + r)
                    send(4 * it + r - 3, 1 + r)
            for q in range(PAIRS - 3, PAIRS):
                send(q, q)

        @block.scalar
        def _(act):
            sc = nc.scalar
            act.wait_ge(m["var_ok"], 1)
            sc.activation(lnb[:, 3, :], lnb[:, 2, :], ACT.Sqrt).then_inc(m["std_ok"], 1)
            act.wait_ge(m["ms_ok"], 1)
            sc.activation(lnb[:, 5, :], lnb[:, 4, :], ACT.Sqrt).then_inc(m["std_ok"], 1)
            act.wait_ge(m["w_in"], 16 * N_W)
            for g in range(GROUPS):
                act.wait_ge(m["xT_ps"], g + 1)
                if g >= 2:
                    act.wait_ge(m["kv_ps"], g - 1)
                sc.activation(xnT[:, g % 2, :], ps[:, g % 2, :], ACT.Copy).then_inc(m["xT_sb"], 1)
                act.wait_ge(m["q_ps"], g + 1)
                sc.activation(q_all[:, g * 512:(g + 1) * 512], ps[:, 2 + g % 2, :], ACT.Identity,
                              scale=sc_col[:, 0:1]).then_inc(m["q_sb"], 1)
            for i in range(4):
                act.wait_ge(m["kst_ps"], i + 1)
                sc.activation(k_stack[:, i * 1024:(i + 1) * 1024], ps[:, 6 + i % 2, :].bitcast(BF16),
                              ACT.Copy).then_inc(m["kst_sb"], 1)
            act.wait_ge(m["e_ok"], 1)
            sc.activation(rs[:, 5, :], rs[:, 4, :], ACT.Exp).then_inc(m["e_exp"], 1)

            def step(u, n):
                if 0 <= n < UNITS:
                    for k in range(CH):
                        act.wait_ge(m["exp_ps"], CH * u + k + 1)
                        if k == 0 and n == 0:
                            act.wait_ge(m["route_ok"], 1)
                        if k == 0 and n >= 2:
                            act.wait_ge(m["pv_ok"], u - 1)
                        sc.activation(probs[:, n % 2, k, :], ex_bank[k % 2], ACT.Exp).then_inc(m["exp_ok"], 1)
                        if k == 0:
                            evac_s(u, n)
                        if k == 1:
                            between(u, n)
                        if k == 3 and n <= UNITS - 2:
                            evac_m(u, n)
                        if k == 6:
                            evac_on(u, n)
                else:
                    evac_s(u, n)
                    between(u, n)
                    if -1 <= n <= UNITS - 2:
                        evac_m(u, n)
                    evac_on(u, n)

            def between(u, n):
                if 0 <= n - 2 < UNITS:
                    act.wait_ge(m["pv_ok"], u - 1)
                    if n - 2 >= 2:
                        act.wait_ge(m["oT_ps"], u - 3)
                    sc.activation(o_T[:, n % 2, :], pv_bank[n % 2], ACT.Copy).then_inc(m["oT_sb"], 1)

            def evac_m(u, n):
                act.wait_ge(m["mT_ps"], u + 2)
                if n + 1 >= 2:
                    act.wait_ge(m_in[(n + 1) % 2], 16 * ((u + 1 - (n + 1) % 2) // 2))
                sc.activation(m_T[:, (n + 1) % 2, :], misc.bitcast(BF16)[0:3 * HU, 0:S], ACT.Copy
                              ).then_inc(m["mT_sb"], 1)

            def evac_on(u, n):
                if n % 2 == 1 and 0 <= n - 3 < UNITS:
                    act.wait_ge(m["onT_ps"], (u - 1) // 2)
                    sc.activation(o_nT[:, :], misc[:, 0:S], ACT.Copy).then_inc(m["onT_sb"], 1)

            def evac_s(u, n):
                if n % 2 == 0 and 0 <= n - 4 < UNITS:
                    act.wait_ge(m["s_ps"], (u - 2) // 2)
                    sc.activation(s_all[:, bass.ds(u - 4, 2), :], misc[:, 0:2 * D].rearrange("p (t d) -> p t d", t=2),
                                  ACT.Copy).then_inc(m["s_ok"], 1)

            attention(act, step)

            act.wait_ge(m["pv_ok"], UNITS)

            def expert(q, n):
                if 0 <= n + 1 < PAIRS:
                    act.wait_ge(m["xsT_ps"], q + 2)
                    if n + 1 >= 2:
                        act.wait_ge(m["h_ps"], q)
                    sc.activation(xT[:, (n + 1) % 2, :], ps[:, 4, 0:256], ACT.Copy).then_inc(m["xsT_sb"], 1)
                if 0 <= n < PAIRS:
                    act.wait_ge(m["g_ok"], q + 1)
                    if n >= 2:
                        act.wait_ge(m["gt_ok"], q - 1)
                    sc.activation(th[:, n % 2, :], glu[:, n % 2, :], ACT.Tanh, scale=ALPHA / 2).then_inc(m["th_ok"], 1)
                if 0 <= n - 2 < PAIRS:
                    act.wait_ge(m["hT_ps"], q - 1)
                    if n - 2 >= 1:
                        act.wait_ge(m["y_ps"], q - 2)
                    sc.activation(hT, ps[:, 5, :], ACT.Copy, scale=0.5).then_inc(m["hT_sb"], 1)
                    act.wait_ge(m["y_ps"], q - 1)
                    act.wait_ge(m["p_ok"], q - 1)
                    if n - 2 >= 4:
                        act.wait_ge(y_out[(n - 2) % 4], 32 * ((q - 2 - (n - 2) % 4) // 4))
                    for t in range(2):
                        sc.activation(ys[:, (n - 2) % 4, t, :], ps[:, 6, t * D:(t + 1) * D], ACT.Identity,
                                      scale=p_st[:, (n - 2) % 4, t:t + 1]).then_inc(m["y_ok"], 1)

            experts(act, expert)

            for g in range(GROUPS):
                act.wait_ge(m["f_ok"], g + 1)
                sc.activation(fb[2 + g % 2].rearrange("p a c -> p (a c)")[:, 0:512],
                              fb[g % 2].rearrange("p a c -> p (a c)")[:, 0:512], ACT.Tanh, scale=0.5
                              ).then_inc(m["fth_ok"], 1)

        @block.tensor
        def _(pe):
            te = nc.tensor
            pe.wait_ge(m["const_in"], 3)
            pe.wait_ge(m["dve"], W24_AT)
            pe.wait_ge(m["w_in"], 16 * N_W)
            for g in range(GROUPS):
                pe.wait_ge(m["xn_ok"], 4 * g + 4)
                if g >= 2:
                    pe.wait_ge(m["xT_sb"], g - 1)
                for t in range(4):
                    last = te.transpose(ps[:, g % 2, t * P:(t + 1) * P], xn_all[:, 4 * g + t, :], ident[:, :])
                last.then_inc(m["xT_ps"], 1)
                pe.wait_ge(m["xT_sb"], g + 1)
                if g >= 2:
                    pe.wait_ge(m["q_sb"], g - 1)
                te.matmul(ps[:, 2 + g % 2, :], wq_sb[:, :], xnT[:, g % 2, :], start=True, stop=True).then_inc(m["q_ps"], 1)
                if g >= 2:
                    pe.wait_ge(m["kv_sb"], g - 1)
                for t in range(4):
                    last = te.matmul(ps[:, 4 + g % 2, t * 24:(t + 1) * 24], xnT[:, g % 2, t * P:(t + 1) * P],
                                     w24_sb[:, :], start=True, stop=True)
                last.then_inc(m["kv_ps"], 1)
            pe.wait_ge(m["krow_ok"], 1)
            for i in range(4):
                if i >= 2:
                    pe.wait_ge(m["kst_sb"], i - 1)
                for t in range(8):
                    last = te.transpose(ps[:, 6 + i % 2, :].bitcast(BF16)[:, t * P:(t + 1) * P],
                                        k_rows[:, 8 * i + t, :], ident_b[:, :])
                last.then_inc(m["kst_ps"], 1)
            pe.wait_ge(m["oh_ok"], 1)
            pe.wait_ge(m["kv_sb"], GROUPS)
            te.matmul(ps[:, 4, 0:256], before[:, :], oh_b[:, :], start=True, stop=True)
            te.matmul(ps[:, 4, 256:512], ones_b[:, :], oh_b[:, :], start=True, stop=True).then_inc(m["rank_ps"], 1)
            pe.wait_ge(m["kst_sb"], 4)
            pe.wait_ge(m["q_sb"], GROUPS)
            pe.wait_ge(m["xT_sb"], GROUPS)

            def scores_exp(u, n, k):
                tt, j = k // 4, k % 4
                if k == 0:
                    pe.wait_ge(m_in[n % 2], 16 * ((u - n % 2) // 2) + 16)
                    pe.wait_ge(ke_in[(n // 2) % 2], 16 * ((u - n % 4) // 4) + 16)
                if n > 0 or k >= 2:
                    pe.wait_ge(m["exp_ok"], CH * u + k - 1)
                te.matmul(ex_bank[k % 2], k_exp[:, (n // 2) % 2, tt * P:(tt + 1) * P],
                          qs[:, n % 4, j * 512:(j + 1) * 512], start=True, stop=True).then_inc(m["exp_ps"], 1)

            def scores_max(u, n, k):
                st, j = k // 4, k % 4
                if k == 0:
                    pe.wait_ge(qs_in[n % 4], 16 * ((u - n % 4) // 4) + 16)
                    pe.wait_ge(km_in[(n // 2) % 2], 16 * ((u - n % 4) // 4) + 16)
                if n > 0 or k >= 2:
                    pe.wait_ge(m["max_ok"], CH * u + k - 1)
                for e in range(2):
                    at = (2 * j + e) * S + st * P
                    last = te.matmul(mx_bank[k % 2][:, e * S:(e + 1) * S], qs[0:MROW, n % 4, at:at + P],
                                     k_max[0:MROW, (n // 2) % 2, :], start=True, stop=True)
                last.then_inc(m["max_ps"], 1)

            def values(v, n, tt):
                if tt == 0:
                    pe.wait_ge(m["exp_ok"], CH * v + CH)
                    pe.wait_ge(v_in[(n // 2) % 2], 16 * ((v - n % 4) // 4) + 16)
                    if n >= 2:
                        pe.wait_ge(m["oT_sb"], v - 1)
                    if n < 1:
                        pe.wait_ge(m["route_ok"], 1)
                for j in range(4):
                    last = te.matmul(pv_bank[n % 2][32 * j:32 * j + 32, :], v_use[:, (n // 2) % 2, tt, :],
                                     probs[:, n % 2, 4 * tt + j, :], start=(tt == 0), stop=(tt == 1))
                if tt == 1:
                    last.then_inc(m["pv_ok"], 1)

            def turn_m(u, n):
                if not -1 <= n <= UNITS - 2:
                    return
                pe.wait_ge(m["mpart"], 5 * (u + 2))
                if n % 2 == 0 and n >= 4:
                    pe.wait_ge(m["s_ok"], (u - 2) // 2)
                elif n >= 0:
                    pe.wait_ge(m["mT_sb"], u + 1)
                for st in range(2):
                    last = te.transpose(misc.bitcast(BF16)[0:3 * HU, st * P:(st + 1) * P],
                                        m_parts[:, (n + 1) % 2, st, :, :].rearrange("p i h -> p (i h)"), ident_b[:, :])
                last.then_inc(m["mT_ps"], 1)

            def turn_o(u, n):
                if 0 <= n - 2 < UNITS:
                    pe.wait_ge(m["oT_sb"], u - 1)
                    if n - 2 >= 1:
                        pe.wait_ge(m["on_ok"], 2 * (u - 2))
                    for i in range(4):
                        last = te.transpose(oT_bank[:, i * P:(i + 1) * P], o_T[:, n % 2, i * P:(i + 1) * P], ident[:, :])
                    last.then_inc(m["oT_ps"], 1)

            def turn_on(u, n):
                if n % 2 == 1 and 0 <= n - 3 < UNITS:
                    pe.wait_ge(m["on_ok"], 2 * (u - 1))
                    pe.wait_ge(m["mT_sb"], (u + 2) if n <= UNITS - 2 else UNITS)
                    for st in range(2):
                        last = te.transpose(misc[:, st * P:(st + 1) * P], o_n[:, st, :], ident[:, :])
                    last.then_inc(m["onT_ps"], 1)

            def project(u, n):
                if n % 2 == 1 and 0 <= n - 3 < UNITS:
                    pe.wait_ge(m["onT_sb"], (u - 1) // 2)
                    for st in range(2):
                        last = te.matmul(misc[:, st * D:(st + 1) * D], o_nT[:, st * P:(st + 1) * P], wout_sb[:, :],
                                         start=True, stop=True)
                    last.then_inc(m["s_ps"], 1)

            def step(u, n):
                for k in range(CH):
                    if 0 <= n < UNITS:
                        scores_exp(u, n, k)
                    if n + 2 < UNITS:
                        scores_max(u + 2, n + 2, k)
                    if k == 2:
                        turn_m(u, n)
                    if k == 1:
                        turn_o(u, n)
                    if k == 3 and 0 <= n - 1 < UNITS:
                        values(u - 1, n - 1, 0)
                    if k == 5:
                        turn_on(u, n)
                    if k == 7:
                        project(u, n)
                        if 0 <= n - 1 < UNITS:
                            values(u - 1, n - 1, 1)

            attention(pe, step)

            pe.wait_ge(m["s_ok"], B)
            pe.wait_ge(m["bias_r"], 16)

            packed = [None, None]

            def expert(q, n):
                if n >= 0 and n % 4 == 0:
                    for h in range(2):
                        if h == 1 or n < PAIRS:
                            packed[h] = pe.value_load(eid_i[0:1, h, bass.ds((q - n % 4) // 4, 1)],
                                                      min_val=0, max_val=8 ** 8 - 1)
                if 0 <= n + 1 < PAIRS:
                    pe.wait_ge(xs_in[(n + 1) % 4], 16 * ((q + 1 - (n + 1) % 4) // 4) + 16)
                    if n + 1 >= 1:
                        pe.wait_ge(m["xsT_sb"], q + 1)
                    for t in range(2):
                        last = te.transpose(ps[:, 4, t * P:(t + 1) * P], xs[:, (n + 1) % 4, t, 0:D], ident[:, :])
                    last.then_inc(m["xsT_ps"], 1)
                if 0 <= n < PAIRS:
                    if n >= 2:
                        pe.wait_ge(m["l_ok"], q - 1)
                    await_ge(pe, m["xsT_sb"], q + 1, m["pe_passed"])
                    for t in range(2):
                        e = pe.snap((packed[0] >> (3 * (2 * (n % 4) + t))) & (E - 1))
                        bank = ps[:, 2 * (n % 2) + t, :]
                        te.matmul(bank, ones_b[0:3, :], bias_rows[:, bass.ds(e * 2 * INNER, 2 * INNER)], start=True, stop=False)
                        last = te.matmul(bank, xT[:, n % 2, t * P:(t + 1) * P], w1_sb[:, bass.ds(e * 2 * INNER, 2 * INNER)],
                                         start=False, stop=True)
                    last.then_inc(m["h_ps"], 1)
                if 0 <= n - 2 < PAIRS:
                    r = n % 2
                    pe.wait_ge(m["hid_ok"], q - 1)
                    if n - 2 >= 1:
                        pe.wait_ge(m["hT_sb"], q - 2)
                    for i in range(4):
                        last = te.transpose(ps[:, 5, i * P:(i + 1) * P], hid[:, r, i * P:(i + 1) * P], ident[:, :])
                    last.then_inc(m["hT_ps"], 1)
                    if n - 2 >= 1:
                        pe.wait_ge(m["y_ok"], 2 * (q - 2))
                    await_ge(pe, m["hT_sb"], q - 1, m["pe_passed"])
                    for t in range(2):
                        e = pe.snap((packed[1] >> (3 * (2 * (n % 4) + t))) & (E - 1))
                        yt = ps[:, 6, t * D:(t + 1) * D]
                        te.matmul(yt, ones_b[0:3, :], bias_rows[:, bass.ds(e * D + E * 2 * INNER, D)], start=True, stop=False)
                        for c in range(2):
                            last = te.matmul(yt, hT[:, (2 * t + c) * P:(2 * t + c + 1) * P],
                                             w2_sb[:, bass.ds(e * 2 * D + c * D, D)], start=False, stop=(c == 1))
                    last.then_inc(m["y_ps"], 1)

            experts(pe, expert)

        @block.vector
        def _(dve):
            ve = nc.vector
            count = [0]

            def link(ins):
                count[0] += 1
                ins.then_inc(m["dve"], 1)
                dve.wait_ge(m["dve"], count[0])

            for g in range(GROUPS):
                dve.wait_ge(m["x_in"], 16 * GROUPS)
                for t in range(4 * g, 4 * g + 4):
                    last = ve.bn_stats(st6[:, t, :], x_all[:, t, :])
            last.then_inc(m["stat"], 1)
            dve.wait_ge(m["stat"], 1)
            for t in range(TILES):
                last = ve.bn_aggr(mv[:, t, :], st6[:, t, :])
            last.then_inc(m["stat"], 1)
            dve.wait_ge(m["stat"], 2)
            ve.tensor_scalar(lnb[:, 2, :], mv[:, :, 1], EPS, None, ALU.add).then_inc(m["var_ok"], 1)
            dve.wait_ge(m["std_ok"], 1)
            link(ve.reciprocal(rstd, lnb[:, 3, :]))
            link(ve.tensor_tensor(lnb[:, 6, :], mv[:, :, 1], rstd, ALU.mult))
            link(ve.tensor_tensor(lnb[:, 7, :], lnb[:, 6, :], rstd, ALU.mult))
            ve.tensor_scalar(lnb[:, 4, :], lnb[:, 7, :], EPS, None, ALU.add).then_inc(m["ms_ok"], 1)
            dve.wait_ge(m["w_in"], 16 * N_W)
            link(ve.tensor_scalar(w24_sb[:, 0:E], w24_sb[:, 0:E], ns_col[:, 0:1], None, ALU.mult))
            assert count[0] == W24_AT
            for t in range(TILES):
                ve.tensor_scalar(xn_all[:, t, :], x_all[:, t, :], mv[:, t, 0:1], lnb[:, 0, t:t + 1],
                                 ALU.subtract, ALU.mult).then_inc(m["xn_ok"], 1)
            dve.wait_ge(m["std_ok"], 2)
            link(ve.reciprocal(rms, lnb[:, 5, :]))
            link(ve.tensor_copy(bias_parts[:, 0, :], bias_in[:, :]))
            link(ve.tensor_tensor(bias_rest[:, 0, :], bias_in[:, :], bias_parts[:, 0, :], ALU.subtract))
            link(ve.tensor_copy(bias_parts[:, 1, :], bias_rest[:, 0, :]))
            ve.tensor_tensor(bias_parts[:, 2, :], bias_rest[:, 0, :], bias_parts[:, 1, :], ALU.subtract).then_inc(m["bias_ok"], 1)
            for g in range(GROUPS):
                dve.wait_ge(m["kv_ps"], g + 1)
                ve.tensor_copy(kvg[:, 4 * g:4 * g + 4, :], ps[:, 4 + g % 2, 0:96].rearrange("p (t c) -> p t c", t=4)
                               ).then_inc(m["kv_sb"], 1)
            dve.wait_ge(m["kv_sb"], GROUPS)
            dve.wait_ge(m["const_in"], 3)
            kf = kvg[:, :, E:E + DK]
            link(ve.tensor_copy(k_p[:, 0, :, :], kf))
            link(ve.tensor_tensor(k_rest[:, 0, :, :], kf, k_p[:, 0, :, :], ALU.subtract))
            link(ve.tensor_copy(k_p[:, 1, :, :], k_rest[:, 0, :, :]))
            link(ve.tensor_tensor(k_p[:, 2, :, :], k_rest[:, 0, :, :], k_p[:, 1, :, :], ALU.subtract))
            for jj in range(3):
                for i in range(3):
                    at = (3 * jj + i) * DK
                    last = ve.tensor_copy(k_rows[:, :, at:at + DK], k_p[:, jj, :, :])
            last.then_inc(m["krow_ok"], 1)
            ve.tensor_copy(v_all[:, :, 0:DK], kvg[:, :, E + DK:24]).then_inc(m["v_ok"], 2)

            def t3(i):
                return rt[:, i, :].rearrange("p (t e) -> p t e", e=E)

            def over_e(col):
                return replicated(col, E, 2)

            def over_t(row):
                return replicated(row, TILES, 1)

            rank = ps[:, 4, 0:256].rearrange("p (t e) -> p t e", e=E)
            tot = ps[:, 4, 256:512].rearrange("p (t e) -> p t e", e=E)
            link(ve.tensor_tensor(t3(0), kvg[:, :, 0:E], over_e(rms), ALU.mult))
            link(ve.tensor_tensor(t3(1), t3(0), over_t(gb_row[:, :]), ALU.add))
            link(ve.tensor_reduce(rs[:, 0, :], t3(1), AX, ALU.max))
            link(ve.tensor_tensor(t3(2), t3(1), over_e(rs[:, 0, :]), ALU.is_equal))
            link(ve.tensor_tensor(t3(3), t3(2), over_t(rev8[:, :]), ALU.mult))
            link(ve.tensor_reduce(rs[:, 1, :], t3(3), AX, ALU.max))
            link(ve.tensor_tensor(t3(4), t3(3), over_e(rs[:, 1, :]), ALU.is_equal))
            link(ve.scalar_tensor_tensor(t3(5), t3(4), -BIG, t3(1), ALU.mult, ALU.add))
            link(ve.tensor_reduce(rs[:, 2, :], t3(5), AX, ALU.max))
            ve.tensor_tensor(rs[:, 4, :], rs[:, 2, :], rs[:, 0, :], ALU.subtract).then_inc(m["e_ok"], 1)
            link(ve.tensor_tensor(t3(6), t3(5), over_e(rs[:, 2, :]), ALU.is_equal))
            link(ve.tensor_tensor(t3(7), t3(6), over_t(rev8[:, :]), ALU.mult))
            link(ve.tensor_reduce(rs[:, 3, :], t3(7), AX, ALU.max))
            link(ve.tensor_tensor(t3(8), t3(7), over_e(rs[:, 3, :]), ALU.is_equal))
            ve.tensor_tensor(oh_b[:, :], rt[:, 4, :], rt[:, 8, :], ALU.add).then_inc(m["oh_ok"], 1)
            dve.wait_ge(m["e_exp"], 1)
            link(ve.tensor_scalar(rs[:, 6, :], rs[:, 5, :], 1.0, None, ALU.add))
            link(ve.reciprocal(rs[:, 7, :], rs[:, 6, :]))
            ve.tensor_copy(meta[:, :, 0, 1], rs[:, 7, :])
            ve.tensor_tensor(meta[:, :, 1, 1], rs[:, 7, :], rs[:, 5, :], ALU.mult)
            dve.wait_ge(m["rank_ps"], 1)
            pad = 16 * E
            link(ve.tensor_copy(scan[:, 0, pad:], ps[:, 4, 256:512]))
            src = 0
            for d in (1, 2, 4, 8, 16):
                link(ve.tensor_tensor(scan[:, 1 - src, pad:], scan[:, src, pad:],
                                      scan[:, src, pad - d * E:pad - d * E + TILES * E], ALU.add))
                src = 1 - src
            incl = scan[:, src, pad:].rearrange("p (t e) -> p t e", e=E)
            counts = scan[:, src, pad + (TILES - 1) * E:]
            link(ve.tensor_tensor(t3(9), incl, tot, ALU.subtract))
            link(ve.tensor_tensor(t3(10), t3(9), rank, ALU.add))
            link(ve.memset(nt[:, :, :], 0.0))
            link(ve.tensor_tensor(cmp_n[:, :, :], replicated(counts, TILES, 2), replicated(steps128[:, :], E, 1), ALU.is_gt))
            link(ve.tensor_reduce(nt[:, 0, 8:16], cmp_n[:, :, :], AX, ALU.add))
            for i, d in enumerate((1, 2, 4)):
                link(ve.tensor_tensor(nt[:, i + 1, 8:16], nt[:, i, 8:16], nt[:, i, 8 - d:16 - d], ALU.add))
            link(ve.tensor_tensor(nt[:, 4, 8:16], nt[:, 3, 8:16], nt[:, 0, 8:16], ALU.subtract))
            link(ve.tensor_scalar(nt[:, 5, 8:16], nt[:, 4, 8:16], float(P), None, ALU.mult))
            link(ve.tensor_tensor(t3(11), t3(10), over_t(nt[:, 5, 8:16]), ALU.add))
            for k, oh in enumerate((4, 8)):
                link(ve.tensor_tensor(t3(9), t3(oh), t3(11), ALU.mult))
                link(ve.tensor_reduce(rs[:, 8 + k, :], t3(9), AX, ALU.add))
                ve.tensor_copy(pos_i[:, :, k], rs[:, 8 + k, :])
            link(ve.tensor_tensor(cmp_t[:, :, :], replicated(tile_no[:, :], E, 2),
                                  replicated(nt[:, 3, 8:16], SORTED, 1), ALU.is_ge))
            link(ve.tensor_reduce(cmp_s[:, :], cmp_t[:, :, :], AX, ALU.add))
            link(ve.tensor_scalar(eid_f[:, 4:4 + SORTED], cmp_s[:, :], float(E - 1), None, ALU.min))
            for h, at in enumerate((4, 0)):
                tiles8 = eid_f[:, at:at + 80].rearrange("p (i j) -> p i j", j=8)
                link(ve.tensor_tensor(eid_p[:, :, :], tiles8, replicated(pow8[:, :], 10, 1), ALU.mult))
                link(ve.tensor_reduce(eid_s[:, h, :], eid_p[:, :, :], AX, ALU.add))
            ve.tensor_copy(eid_i[:, :, :], eid_s[0:1, :, :]).then_inc(m["route_ok"], 1)

            def normalise(u, n):
                if not 0 <= n - 2 < UNITS:
                    return
                c = n % 2
                ov = oT_bank.rearrange("p (e t j d) -> p e t j d", e=2, t=2, j=4)
                dve.wait_ge(m["oT_ps"], u - 1)
                if n >= 3:
                    dve.wait_ge(m["on_ok"], 2 * (u - 2))
                ve.reciprocal(inv_sum[:, c, :, :], oT_bank.rearrange("p (i j d) -> p i j d", i=4, j=4)[:, :, :, DK]
                              ).then_inc(m["inv_ok"], 1)
                dve.wait_ge(m["inv_ok"], u - 1)
                if c == 0 and n >= 4:
                    dve.wait_ge(m["onT_ps"], (u - 2) // 2)
                for st in range(2):
                    dst = o_n[:, st, :].rearrange("p (c j e d) -> p c e j d", c=2, j=4, e=2)[:, c, :, :, :]
                    inv = inv_sum[:, c, :, :].rearrange("p (e t) j -> p e t j", e=2)[:, :, st, :]
                    ve.tensor_tensor(dst, ov[:, :, st, :, 0:DK], replicated(inv, DK, 3), ALU.mult
                                     ).then_inc(m["on_ok"], 1)

            def split_m(u, n):
                r = n % 2
                mx = maxes[:, r, :, :]
                dve.wait_ge(m["max_ok"], CH * u + CH)
                if n >= 2:
                    dve.wait_ge(m["mT_ps"], u - 1)
                ve.tensor_scalar(m_parts[:, r, :, 0, :], mx, -1.0, None, ALU.mult).then_inc(m["mpart"], 1)
                dve.wait_ge(m["mpart"], 5 * u + 1)
                ve.tensor_tensor(m_rest[:, r, 0, :, :], mx, m_parts[:, r, :, 0, :], ALU.add).then_inc(m["mpart"], 1)
                dve.wait_ge(m["mpart"], 5 * u + 2)
                ve.tensor_scalar(m_parts[:, r, :, 1, :], m_rest[:, r, 0, :, :], -1.0, None, ALU.mult).then_inc(m["mpart"], 1)
                dve.wait_ge(m["mpart"], 5 * u + 3)
                ve.tensor_tensor(m_rest[:, r, 1, :, :], m_rest[:, r, 0, :, :], m_parts[:, r, :, 1, :], ALU.add).then_inc(m["mpart"], 1)
                dve.wait_ge(m["mpart"], 5 * u + 4)
                ve.tensor_scalar(m_parts[:, r, :, 2, :], m_rest[:, r, 1, :, :], -1.0, None, ALU.mult).then_inc(m["mpart"], 1)

            def step(u, n):
                if n + 2 < UNITS:
                    for k in range(CH):
                        st, j = k // 4, k % 4
                        dve.wait_ge(m["max_ps"], CH * (u + 2) + k + 1)
                        ve.tensor_reduce(maxes[:, n % 2, st, 2 * j:2 * j + 2],
                                         mx_bank[k % 2].rearrange("p (e t) -> p e t", e=2), AX, ALU.max
                                         ).then_inc(m["max_ok"], 1)
                        if k == 3:
                            normalise(u, n)
                    split_m(u + 2, n + 2)
                else:
                    normalise(u, n)

            attention(dve, step)
            dve.wait_ge(m["pv_ok"], UNITS)

            def expert(q, n):
                if not 0 <= n < PAIRS:
                    return
                r = n % 2
                hb = ps[:, 2 * r:2 * r + 2, :]
                g3 = glu[:, r, :].rearrange("p (t c) -> p t c", t=2)
                l3 = lin[:, r, :].rearrange("p (t c) -> p t c", t=2)
                dve.wait_ge(m["h_ps"], q + 1)
                if n >= 2:
                    dve.wait_ge(m["gt_ok"], q - 1)
                    dve.wait_ge(m["hid_ok"], q - 1)
                ve.tensor_scalar(g3, hb[:, :, 0:INNER], LIMIT, None, ALU.min).then_inc(m["g_ok"], 1)
                ve.tensor_scalar(l3, hb[:, :, INNER:], LIMIT, -LIMIT, ALU.min, ALU.max).then_inc(m["l_ok"], 1)
                dve.wait_ge(m["g_ok"], q + 1)
                dve.wait_ge(m["th_ok"], q + 1)
                ve.scalar_tensor_tensor(gt[:, r, :], th[:, r, :], 1.0, glu[:, r, :], ALU.add, ALU.mult).then_inc(m["gt_ok"], 1)
                dve.wait_ge(m["gt_ok"], q + 1)
                dve.wait_ge(m["l_ok"], q + 1)
                if n >= 2:
                    dve.wait_ge(m["hT_ps"], q - 1)
                ve.scalar_tensor_tensor(hid[:, r, :], lin[:, r, :], 1.0, gt[:, r, :], ALU.add, ALU.mult).then_inc(m["hid_ok"], 1)

            experts(dve, expert)

            fin = [0]

            def linkf(ins):
                fin[0] += 1
                ins.then_inc(m["dve"], 1)
                dve.wait_ge(m["dve"], count[0] + fin[0])

            def add_up(g):
                f = fb[g % 2].rearrange("p a c -> p (a c)")[:, 0:512].rearrange("p (t d) -> p t d", t=4)
                dve.wait_ge(yb_in[g % 4], 16 * (g // 4) + 16)
                if g >= 2:
                    dve.wait_ge(m["o_ok"], g - 1)
                linkf(ve.tensor_tensor(f, xn_all[:, 4 * g:4 * g + 4, :], yb[:, g % 4, :, 0:D], ALU.add))
                ve.tensor_tensor(f, f, yb[:, g % 4, :, D:2 * D], ALU.add).then_inc(m["f_ok"], 1)

            add_up(0)
            for g in range(GROUPS):
                if g + 1 < GROUPS:
                    add_up(g + 1)
                f = fb[g % 2].rearrange("p a c -> p (a c)")[:, 0:512].rearrange("p (t d) -> p t d", t=4)
                tf = fb[2 + g % 2].rearrange("p a c -> p (a c)")[:, 0:512].rearrange("p (t d) -> p t d", t=4)
                xg = x_all[:, 4 * g:4 * g + 4, :]
                dve.wait_ge(m["f_ok"], g + 1)
                dve.wait_ge(m["fth_ok"], g + 1)
                linkf(ve.scalar_tensor_tensor(f, tf, 1.0, f, ALU.add, ALU.mult))
                linkf(ve.scalar_tensor_tensor(f, f, 0.5, s_all[:, 4 * g:4 * g + 4, :], ALU.mult, ALU.mult))
                ve.tensor_tensor(xg, xg, f, ALU.add).then_inc(m["o_ok"], 1)


W24_AT = 4


def kernel(L0_attn_x, L0_attn_w_q, L0_attn_w_k, L0_attn_w_v, L0_attn_w_out, L0_attn_softmax_scale,
           L0_ffn_norm_scale, L0_ffn_gate_w, L0_ffn_gate_b, L0_ffn_mlp1_w, L0_ffn_mlp1_b, L0_ffn_mlp2_w,
           L0_ffn_mlp2_b):
    import concourse.bacc as bacc
    from concourse.bass_utils import run_bass_kernel_spmd

    order = [4 * j + 2 * c + e for c in range(2) for j in range(4) for e in range(2)]
    a = {}
    a["x"] = np.ascontiguousarray(L0_attn_x).reshape(TOKENS, D)
    wq = np.asarray(L0_attn_w_q).reshape(HEADS, DK, D)[order]
    a["wq"] = np.ascontiguousarray(wq.transpose(2, 1, 0).reshape(D, D))
    a["w24"] = np.ascontiguousarray(np.concatenate(
        [np.asarray(L0_ffn_gate_w), np.asarray(L0_attn_w_k).T, np.asarray(L0_attn_w_v).T], axis=1))
    wo = np.asarray(L0_attn_w_out).reshape(D, HEADS, DK)[:, order]
    a["wout"] = np.ascontiguousarray(wo.reshape(D, D).T)
    a["nscale"] = np.ascontiguousarray(L0_ffn_norm_scale)
    a["gate_b"] = np.ascontiguousarray(L0_ffn_gate_b)
    w1 = np.asarray(L0_ffn_mlp1_w).reshape(E, D, INNER, 2)
    a["w1"] = np.ascontiguousarray(w1.transpose(1, 0, 3, 2).reshape(D, E * 2 * INNER))
    a["b1"] = np.ascontiguousarray(np.asarray(L0_ffn_mlp1_b).reshape(E, INNER, 2).transpose(0, 2, 1).reshape(-1))
    w2 = np.asarray(L0_ffn_mlp2_w).reshape(E, 2, P, D)
    a["w2"] = np.ascontiguousarray(w2.transpose(2, 0, 1, 3).reshape(P, E * 2 * D))
    a["b2"] = np.ascontiguousarray(L0_ffn_mlp2_b).reshape(-1)
    a["scale"] = np.ascontiguousarray(L0_attn_softmax_scale)

    nc = bacc.Bacc("TRN2", target_bir_lowering=False, num_devices=1)
    arrays = {f"in_{k}": v for k, v in a.items()}
    args = [nc.dram_tensor(k, v.shape, mybir.dt.from_np(v.dtype), kind="ExternalInput").ap() for k, v in arrays.items()]
    out = nc.dram_tensor("out_0", (TOKENS, D), F32, kind="ExternalOutput").ap()
    build(nc, *args, out)
    res = run_bass_kernel_spmd(nc, [arrays], core_ids=[0])
    return res.results[0]["out_0"].reshape(B, S, D)
```

```python
from contextlib import ExitStack

import numpy as np
import concourse.bass as bass
from concourse import mybir
from concourse.alu_op_type import AluOpType as ALU

ACT = mybir.ActivationFunctionType
F32 = mybir.dt.float32
BF16 = mybir.dt.bfloat16
I32 = mybir.dt.int32
AX = mybir.AxisListType.X

P = 128
B, S, D = 16, 256, 128
HEADS = 16
DK = D // HEADS
TOKENS = B * S
TILES = TOKENS // P
GROUPS = TILES // 4
E, INNER, TOPK = 8, 256, 2
LIMIT, ALPHA, EPS = 7.0, 1.702, 1e-5
UNITS = 2 * B
HU = HEADS // 2
UCOLS = HU * S
CH = 8
KROWS = 9 * DK
MROW = 96
SORTED = TOPK * TOKENS // P + E
PAIRS = SORTED // 2
ROW = D + 4
BIG = 3.0e38


def replicated(ap, times, at):
    dims = [list(d) for d in ap.ap]
    return bass.AP(ap.tensor, ap.offset, dims[:at] + [[0, times]] + dims[at:])


def await_ge(eng, semaphore, value, passed):
    eng.wait_ge(semaphore, value)
    if not isinstance(value, int):
        eng.sem_inc(passed, 1)


def build(nc, x, wq, w24, wout, nscale, gate_b, w1, b1, w2, b2, scale, out):
    ctx = ExitStack()
    with ctx:
        def sb(name, shape, dt=F32):
            return ctx.enter_context(nc.sbuf_tensor(name, shape, dt))

        def sem(name):
            return ctx.enter_context(nc.semaphore(name))

        q_dram = nc.dram_tensor("q_dram", [B, 3, P, S], BF16, kind="Internal").ap()
        bias_dram = nc.dram_tensor("bias_dram", [3, E * 2 * INNER + E * D], BF16, kind="Internal").ap()
        sorted_dram = nc.dram_tensor("sorted_dram", [SORTED * P, ROW], F32, kind="Internal").ap()
        y_dram = nc.dram_tensor("y_dram", [TOPK * TOKENS + SORTED * P, D], F32, kind="Internal").ap()

        x_all = sb("x_all", [P, TILES, D])
        xn_all = sb("xn_all", [P, TILES, D])
        s_all = sb("s_all", [P, TILES, D])
        w1_sb = sb("w1_sb", [P, E * 2 * INNER])
        w2_sb = sb("w2_sb", [P, E * 2 * D])
        bias_rows = sb("bias_rows", [3, E * 2 * INNER + E * D], BF16)
        wq_sb = sb("wq_sb", [P, D])
        wout_sb = sb("wout_sb", [P, D])
        w24_sb = sb("w24_sb", [P, 24])
        ns_col = sb("ns_col", [P, 1])
        ns_row = sb("ns_row", [P, D])
        gb_row = sb("gb_row", [P, E])
        sc_col = sb("sc_col", [P, 1])
        bias_in = sb("bias_in", [P, 40])
        bias_rest = sb("bias_rest", [P, 2, 40])
        bias_parts = sb("bias_parts", [P, 3, 40], BF16)
        ident = sb("ident", [P, P])
        ident_b = sb("ident_b", [P, P], BF16)
        before = sb("before", [P, P], BF16)
        ones_b = sb("ones_b", [P, P], BF16)
        ones_f = sb("ones_f", [P, P])
        rev8 = sb("rev8", [P, E])
        steps128 = sb("steps128", [P, TILES])
        tile_no = sb("tile_no", [P, SORTED])
        meta = sb("meta", [P, TILES, TOPK, 2])
        pad_row = sb("pad_row", [P, ROW])
        st6 = sb("st6", [P, TILES, 6])
        mv = sb("mv", [P, TILES, 2])
        lnb = sb("lnb", [P, 8, TILES])
        rstd, rms = lnb[:, 0, :], lnb[:, 1, :]
        xnT = sb("xnT", [P, 2, 512])
        q_all = sb("q_all", [P, TOKENS])
        q_parts = sb("q_parts", [P, 2, 3, 512], BF16)
        q_rest = sb("q_rest", [P, 2, 512])
        kvg = sb("kvg", [P, TILES, 24])
        k_p = sb("k_p", [P, 3, TILES, DK], BF16)
        k_stack = sb("k_stack", [P, TOKENS], BF16)
        v_all = sb("v_all", [P, TILES, 32])
        qs = sb("qs", [P, 4, UCOLS], BF16)
        k_max = sb("k_max", [P, 2, S], BF16)
        k_exp = sb("k_exp", [P, 2, S], BF16)
        v_use = sb("v_use", [P, 2, 2, 32])
        probs = sb("probs", [P, 2, CH, 512])
        maxes = sb("maxes", [P, 2, 2, HU])
        m_rest = sb("m_rest", [P, 2, 2, 2, HU])
        m_parts = sb("m_parts", [P, 2, 2, 3, HU], BF16)
        m_T = sb("m_T", [3 * HU, 2, S], BF16)
        o_T = sb("o_T", [P, 2, 512])
        inv_sum = sb("inv_sum", [P, 2, 4, 4])
        o_n = sb("o_n", [P, 2, D])
        o_nT = sb("o_nT", [P, S])
        rs = sb("rs", [P, 10, TILES])
        oh_b = sb("oh_b", [P, TILES * E], BF16)
        nt = sb("nt", [P, 6, 16])
        pos_i = sb("pos_i", [P, TILES, TOPK], I32)
        eid_f = sb("eid_f", [P, SORTED + 16])
        pow8 = sb("pow8", [P, 8])
        eid_p = sb("eid_p", [P, 10, 8])
        eid_s = sb("eid_s", [P, 2, 10])
        eid_i = sb("eid_i", [1, 2, 10], I32)
        pf = probs[:, :, :, :].rearrange("p a b c -> p (a b c)")
        rt = s_all[:, 8:TILES, :].rearrange("p (i t) d -> p i (t d)", t=2)
        scan = w1_sb[:, 0:768].rearrange("p (i c) -> p i c", i=2)
        cmp_n = w1_sb[:, 768:1024].rearrange("p (e t) -> p e t", e=E)
        cmp_t = w1_sb[:, 1024:1600].rearrange("p (t e) -> p t e", e=E)
        cmp_s = w1_sb[:, 1600:1672]
        k_rest = pf[:, 4672:5184].rearrange("p (i t d) -> p i t d", i=2, d=DK)
        k_rows = pf[:, 5184:7232].bitcast(BF16).rearrange("p (t c) -> p t c", c=P)
        t_raw = sb("t_raw", [P, 2, D])
        r_col = sb("r_col", [P, 2, 1])
        pos_st = sb("pos_st", [P, 2, TOPK], I32)
        row_st = sb("row_st", [P, 2, TOPK, ROW])
        xs = sb("xs", [P, 4, 2, ROW])
        xT = pf[:, 0:512].rearrange("p (a c) -> p a c", a=2)
        glu = pf[:, 512:1536].rearrange("p (a c) -> p a c", a=2)
        lin = pf[:, 1536:2560].rearrange("p (a c) -> p a c", a=2)
        th = pf[:, 2560:3584].rearrange("p (a c) -> p a c", a=2)
        gt = pf[:, 3584:4608].rearrange("p (a c) -> p a c", a=2)
        hid = pf[:, 4608:5632].rearrange("p (a c) -> p a c", a=2)
        hT = pf[:, 5632:6144]
        ys = pf[:, 6144:7168].rearrange("p (a t c) -> p a t c", a=4, t=2)
        pad_at = sb("pad_at", [P, 4, 2])
        p_st = sb("p_st", [P, 4, 2])
        dest_i = sb("dest_i", [P, 4, 2], I32)
        yb = q_all[:, :].rearrange("p (a t c) -> p a t c", a=4, t=4)
        fb = [qs[:, i, :].bitcast(F32).rearrange("p (a c) -> p a c", a=2) for i in range(4)]

        ps = ctx.enter_context(nc.psum_tensor("ps", [P, 8, 512], F32))
        ex_bank = [ps[:, 0, :], ps[:, 1, :]]
        mx_bank = [ps[:, 2, :], ps[:, 3, :]]
        pv_bank = [ps[:, 4, :], ps[:, 5, :]]
        oT_bank = ps[:, 6, :]
        misc = ps[:, 7, :]

        names = """x_in0 x_in1 x_in2 x_in3 w_in w2_in w1_in w24_ok pad_in const_in stat var_ok std_ok ms_ok rms_ok xn_ok xT_ps xT_sb q_ps q_sb kv_ps kv_sb
            krow_ok kst_ps kst_sb v_ok bias_ok bias_w bias_r dve ones_in
            qpart q_w0 q_w1 qs_in0 qs_in1 qs_in2 qs_in3 km_in0 km_in1 ke_in0 ke_in1 v_in0 v_in1
            max_ps max_ok mpart mT_ps mT_sb m_in0 m_in1 exp_ps exp_ok pv_ok oT_sb oT_ps inv_ok on_ok onT_ps onT_sb
            s_ps s_ok oh_ok rank_ps rank_sb e_ok e_exp route_ok prow pool_row scat0 scat1
            xs_in0 xs_in1 xs_in2 xs_in3 xsT_ps xsT_sb h_ps g_ok l_ok th_ok gt_ok hid_ok hT_ps hT_sb y_ps y_ok dest_ok p_ok y_out0 y_out1 y_out2 y_out3
            yb_in0 yb_in1 yb_in2 yb_in3 f_ok fth_ok o_ok out_done pool_passed sp_passed pe_passed""".split()
        m = {n: sem(n) for n in names}
        q_w = [m["q_w0"], m["q_w1"]]
        qs_in = [m[f"qs_in{i}"] for i in range(4)]
        km_in, ke_in, v_in = ([m[f"{n}_in{i}"] for i in range(2)] for n in ("km", "ke", "v"))
        m_in = [m["m_in0"], m["m_in1"]]
        xs_in = [m[f"xs_in{i}"] for i in range(4)]
        yb_in = [m[f"yb_in{i}"] for i in range(4)]
        scat = [m["scat0"], m["scat1"]]
        y_out = [m[f"y_out{i}"] for i in range(4)]
        x_in = [m[f"x_in{i}"] for i in range(4)]
        N_W = 9
        QT = TILES // 4

        def attention(eng, step):
            for u in range(-2, 4):
                step(u, u)
            with eng.Fori(1, UNITS // 4 - 1) as it:
                for r in range(4):
                    step(4 * it + r, 4 + r)
            for u in range(UNITS - 4, UNITS + 3):
                step(u, u)

        def experts(eng, step):
            for q in range(-1, 8):
                step(q, q)
            with eng.Fori(2, PAIRS // 4 - 1) as it:
                for r in range(4):
                    step(4 * it + r, 8 + r)
            for q in range(PAIRS - 4, PAIRS + 2):
                step(q, q)

        block = ctx.enter_context(nc.Block())

        @block.sync
        def _(sp):
            xv = x.rearrange("(t p) d -> p t d", p=P)
            for h in range(4):
                sp.dma_start(x_all[:, QT * h:QT * h + QT, :], xv[:, QT * h:QT * h + QT, :]).then_inc(x_in[h], 16)
            sp.dma_start(w2_sb[:, :], w2).then_inc(m["w2_in"], 16)
            def write_q(g, r):
                await_ge(sp, m["qpart"], 4 * g + 4, m["sp_passed"])
                for b in range(2):
                    sp.dma_start(q_dram[bass.ds(2 * g + b, 1)].rearrange("a i p s -> p (a i) s"),
                                 q_parts[:, r, :, b * S:(b + 1) * S]).then_inc(q_w[r], 16)

            def load_q(u, n, g, gn):
                await_ge(sp, q_w[gn % 2], 32 * (g // 2) + 32, m["sp_passed"])
                if n >= 4:
                    await_ge(sp, m["exp_ps"], CH * (u - 3), m["sp_passed"])
                src = q_dram[bass.ds(2 * g + (n % 4) // 2, 1)].rearrange("a i (d h) s -> (a i d) (h s)", d=DK)
                src = src[:, (n % 2) * UCOLS:(n % 2 + 1) * UCOLS]
                sp.dma_start(qs[0:KROWS, n % 4, :], replicated(src, 3, 0)).then_inc(qs_in[n % 4], 16)

            def load_k(dst, b, s):
                sp.dma_start(dst, k_stack[:, bass.ds(b * S, S)]).then_inc(s, 16)

            def load_v(b, n):
                sp.dma_start(v_use[:, n % 2, :, :], v_all[:, bass.ds(2 * b, 2), :]).then_inc(v_in[n % 2], 16)

            await_ge(sp, m["ones_in"], 1, m["sp_passed"])
            write_q(0, 0)
            for u in range(3):
                load_q(u, u, 0, 0)
            await_ge(sp, m["kst_sb"], 4, m["sp_passed"])
            await_ge(sp, m["v_ok"], 2, m["sp_passed"])
            load_k(k_max[:, 0, :], 0, km_in[0])
            load_k(k_max[:, 1, :], 1, km_in[1])
            load_k(k_exp[:, 0, :], 0, ke_in[0])
            load_v(0, 0)
            sp.wait_ge(m["const_in"], 1)
            sp.dma_start(sorted_dram.rearrange("(t p) c -> p t c", p=P),
                         replicated(pad_row[:, :], SORTED, 1)).then_inc(m["pad_in"], 16)

            def load_late_weights():
                sp.wait_ge(m["route_ok"], 1)
                sp.dma_start(w1_sb[:, :], w1).then_inc(m["w1_in"], 16)
                sp.wait_ge(m["bias_ok"], 1)
                n1 = E * 2 * INNER
                sp.dma_start(bias_dram[:, 0:n1].rearrange("i (p c) -> p i c", p=P),
                             bias_parts[:, :, 0:32]).then_inc(m["bias_w"], 16)
                sp.dma_start(bias_dram[:, n1:].rearrange("i (p c) -> p i c", p=P),
                             bias_parts[:, :, 32:40]).then_inc(m["bias_w"], 16)
                sp.wait_ge(m["bias_w"], 32)
                sp.dma_start(bias_rows[:, :], bias_dram).then_inc(m["bias_r"], 16)

            def turn(u, n):
                if n >= 0:
                    loads(u, n)
                if -1 <= n <= UNITS - 2:
                    await_ge(sp, m["mT_sb"], u + 2, m["sp_passed"])
                    sp.dma_start(qs[MROW:MROW + 3, (n + 1) % 4, :], m_T[:, (n + 1) % 2, :]
                                 ).then_inc(m_in[(n + 1) % 2], 16)

            def loads(u, n):
                if n % 4 == 0 and n + 4 < UNITS:
                    write_q(u // 4 + 1, (n // 4 + 1) % 2)
                if n + 3 < UNITS:
                    load_q(u + 3, n + 3, (u - n % 4) // 4 + (n % 4 + 3) // 4, n // 4 + (n % 4 + 3) // 4)
                if n % 2 == 0 and n // 2 + 2 < B:
                    await_ge(sp, m["max_ps"], CH * (u + 2), m["sp_passed"])
                    load_k(k_max[:, (n // 2) % 2, :], (u - n % 2) // 2 + 2, km_in[(n // 2) % 2])
                if n % 2 == 0 and n // 2 + 1 < B:
                    if n >= 2:
                        await_ge(sp, m["exp_ps"], CH * u, m["sp_passed"])
                    load_k(k_exp[:, (n // 2 + 1) % 2, :], (u - n % 2) // 2 + 1, ke_in[(n // 2 + 1) % 2])
                if n % 2 == 1 and n // 2 + 1 < B:
                    if n >= 3:
                        await_ge(sp, m["pv_ok"], u - 1, m["sp_passed"])
                    load_v((u - 1) // 2 + 1, n // 2 + 1)

            for u in range(-1, 8):
                turn(u, u)
            load_late_weights()
            with sp.Fori(1, 3) as it:
                for r in range(8):
                    turn(8 * it + r, 8 + r)
            for u in range(24, UNITS):
                turn(u, u)

            await_ge(sp, scat[0], 8 * TOPK * TILES, m["sp_passed"])

            await_ge(sp, scat[1], 8 * TOPK * TILES, m["sp_passed"])

            def load_sorted(q, n):
                if n >= 4:
                    await_ge(sp, m["xsT_ps"], q - 3, m["sp_passed"])
                    await_ge(sp, m["p_ok"], q - 3, m["sp_passed"])
                    await_ge(sp, m["dest_ok"], 3 * (q - 3), m["sp_passed"])
                sp.dma_start(xs[:, n % 4, :, :],
                             sorted_dram[bass.ds(q * 2 * P, 2 * P), :].rearrange("(t p) c -> p t c", p=P)
                             ).then_inc(xs_in[n % 4], 16)

            for q in range(4):
                load_sorted(q, q)
            with sp.Fori(1, PAIRS // 4) as it:
                for r in range(4):
                    load_sorted(4 * it + r, 4 + r)

            for r in range(4):
                await_ge(sp, y_out[r], 4 * SORTED, m["sp_passed"])
            yv = y_dram[0:TOPK * TOKENS, :].rearrange("(t p k) d -> p t (k d)", p=P, k=TOPK)
            ov = out.rearrange("(t p) d -> p t d", p=P)
            for g in range(4):
                sp.dma_start(yb[:, g, :, :], yv[:, 4 * g:4 * g + 4, :]).then_inc(yb_in[g], 16)
            for g in range(GROUPS):
                await_ge(sp, m["o_ok"], g + 1, m["sp_passed"])
                sp.dma_start(ov[:, 4 * g:4 * g + 4, :], x_all[:, 4 * g:4 * g + 4, :]).then_inc(m["out_done"], 16)
                if g + 4 < GROUPS:
                    sp.dma_start(yb[:, g, :, :], yv[:, 4 * g + 16:4 * g + 20, :]).then_inc(yb_in[g], 16)
            await_ge(sp, m["out_done"], 16 * GROUPS, m["sp_passed"])

        @block.gpsimd
        def _(pool):
            gp = nc.gpsimd
            count = [0]

            def link(ins):
                count[0] += 1
                ins.then_inc(m["prow"], 1)
                await_ge(pool, m["prow"], count[0], m["pool_passed"])

            link(gp.memset(pad_row[:, :], 0.0))
            link(gp.memset(pad_row[:, D + 2:D + 3], float(P)))
            gp.iota(pad_row[:, D:D + 1], pattern=[[0, 1]], base=TOPK * TOKENS, channel_multiplier=1,
                    allow_small_or_imprecise_dtypes=True).then_inc(m["const_in"], 1)
            link(gp.memset(ones_f[:, :], 1.0))
            gp.memset(ones_b[:, :], 1.0)
            link(gp.affine_select(out=ident[:, :], in_=ones_f[:, :], compare_op=ALU.is_equal, fill=0.0, base=0,
                                  pattern=[[-1, P]], channel_multiplier=1))
            gp.tensor_copy(ident_b[:, :], ident[:, :])
            gp.affine_select(out=before[:, :], in_=ones_f[:, :], compare_op=ALU.is_gt, fill=0.0, base=0,
                             pattern=[[1, P]], channel_multiplier=-1)
            gp.iota(rev8[:, :], pattern=[[-1, E]], base=E, channel_multiplier=0, allow_small_or_imprecise_dtypes=True)
            gp.iota(steps128[:, :], pattern=[[P, TILES]], base=0, channel_multiplier=0,
                    allow_small_or_imprecise_dtypes=True)
            gp.iota(tile_no[:, :], pattern=[[1, SORTED]], base=0, channel_multiplier=0,
                    allow_small_or_imprecise_dtypes=True)
            gp.iota(meta[:, :, :, 0], pattern=[[TOPK * P, TILES], [1, TOPK]], base=0, channel_multiplier=TOPK,
                    allow_small_or_imprecise_dtypes=True)
            gp.memset(row_st[:, :, :, :], 0.0)
            gp.memset(eid_f[:, :], 0.0)
            for i in range(8):
                gp.memset(pow8[:, i:i + 1], float(8 ** i))
            gp.memset(scan[:, :, :], 0.0)
            gp.memset(k_rows[:, :, KROWS:P], 0.0).then_inc(m["const_in"], 1)
            await_ge(pool, m["const_in"], 2, m["pool_passed"])
            gp.memset(k_rows[:, :, MROW:MROW + 3], 1.0)
            link(gp.memset(v_all[:, :, :], 0.0))
            gp.memset(v_all[:, :, DK:DK + 1], 1.0).then_inc(m["const_in"], 1)
            gp.memset(qs[:, :, :].bitcast(F32), 0.0).then_inc(m["ones_in"], 1)

            def split_q(g, n):
                r = n % 2
                qv = q_all[:, bass.ds(g * 512, 512)]
                await_ge(pool, m["q_sb"], g + 1, m["pool_passed"])
                if n >= 2:
                    await_ge(pool, q_w[r], 32 * ((g - r) // 2), m["pool_passed"])
                gp.tensor_copy(q_parts[:, r, 0, :], qv).then_inc(m["qpart"], 1)
                await_ge(pool, m["qpart"], 4 * g + 1, m["pool_passed"])
                gp.tensor_tensor(q_rest[:, r, :], qv, q_parts[:, r, 0, :], ALU.subtract).then_inc(m["qpart"], 1)
                await_ge(pool, m["qpart"], 4 * g + 2, m["pool_passed"])
                gp.tensor_copy(q_parts[:, r, 1, :], q_rest[:, r, :]).then_inc(m["qpart"], 1)
                await_ge(pool, m["qpart"], 4 * g + 3, m["pool_passed"])
                gp.tensor_tensor(q_parts[:, r, 2, :], q_rest[:, r, :], q_parts[:, r, 1, :],
                                 ALU.subtract).then_inc(m["qpart"], 1)

            PER = 6

            def scatter(t, n):
                r = n % 2
                done = PER * t
                if n >= 2:
                    await_ge(pool, scat[r], 32 * ((t - r) // 2), m["pool_passed"])
                gp.tensor_copy(r_col[:, r, :], lnb[:, 1, bass.ds(t, 1)]).then_inc(m["pool_row"], 1)
                gp.tensor_tensor(t_raw[:, r, :], xn_all[:, bass.ds(t, 1), :].rearrange("p a d -> p (a d)"),
                                 ns_row[:, :], ALU.mult).then_inc(m["pool_row"], 1)
                gp.tensor_copy(pos_st[:, r, :], pos_i[:, bass.ds(t, 1), :].rearrange("p a k -> p (a k)")
                               ).then_inc(m["pool_row"], 1)
                gp.tensor_copy(row_st[:, r, :, D:D + 2], meta[:, bass.ds(t, 1), :, :].rearrange("p a k c -> p (a k) c")
                               ).then_inc(m["pool_row"], 1)
                await_ge(pool, m["pool_row"], done + 4, m["pool_passed"])
                for k in range(TOPK):
                    gp.tensor_scalar(row_st[:, r, k, 0:D], t_raw[:, r, :], r_col[:, r, :], 1.0,
                                     ALU.mult, ALU.mult).then_inc(m["pool_row"], 1)
                await_ge(pool, m["pool_row"], done + PER, m["pool_passed"])
                for k in range(TOPK):
                    gp.indirect_dma_start(out=sorted_dram, out_offset=bass.IndirectOffsetOnAxis(ap=pos_st[:, r, k:k + 1], axis=0),
                                          in_=row_st[:, r, k, :], in_offset=None).then_inc(scat[r], 16)

            split_q(0, 0)
            split_q(1, 1)
            await_ge(pool, m["route_ok"], 1, m["pool_passed"])
            await_ge(pool, m["pad_in"], 16, m["pool_passed"])
            await_ge(pool, m["w_in"], 16 * N_W, m["pool_passed"])
            for t in range(4):
                scatter(t, t)
            with pool.Fori(1, GROUPS // 2) as it:
                for h in range(2):
                    split_q(2 * it + h, 2 + h)
                    for r in range(4):
                        scatter(8 * it + 4 * h + r - 4, 4 + r)
            for t in range(TILES - 4, TILES):
                scatter(t, t)

            def prepare(q, n):
                r = n % 4
                await_ge(pool, xs_in[r], 16 * ((q - r) // 4) + 16, m["pool_passed"])
                if n >= 4:
                    await_ge(pool, y_out[r], 32 * ((q - r) // 4), m["pool_passed"])
                gp.tensor_tensor(pad_at[:, r, :], xs[:, r, :, D + 2], tile_no[:, bass.ds(2 * q, 2)], ALU.mult
                                 ).then_inc(m["dest_ok"], 1)
                await_ge(pool, m["dest_ok"], 3 * q + 1, m["pool_passed"])
                gp.tensor_tensor(pad_at[:, r, :], xs[:, r, :, D], pad_at[:, r, :], ALU.add).then_inc(m["dest_ok"], 1)
                await_ge(pool, m["dest_ok"], 3 * q + 2, m["pool_passed"])
                if n >= 4:
                    await_ge(pool, m["y_ok"], 2 * (q - 3), m["pool_passed"])
                gp.tensor_copy(p_st[:, r, :], xs[:, r, :, D + 1]).then_inc(m["p_ok"], 1)
                gp.tensor_copy(dest_i[:, r, :], pad_at[:, r, :]).then_inc(m["dest_ok"], 1)
                await_ge(pool, m["dest_ok"], 3 * q + 3, m["pool_passed"])

            def send(q, n):
                r = n % 4
                await_ge(pool, m["y_ok"], 2 * q + 2, m["pool_passed"])
                for t in range(2):
                    gp.indirect_dma_start(out=y_dram, out_offset=bass.IndirectOffsetOnAxis(ap=dest_i[:, r, t:t + 1], axis=0),
                                          in_=ys[:, r, t, :], in_offset=None).then_inc(y_out[r], 16)

            for q in range(3):
                prepare(q, q)
            prepare(3, 3)
            send(0, 0)
            with pool.Fori(1, PAIRS // 4) as it:
                for r in range(4):
                    prepare(4 * it + r, 4 + r)
                    send(4 * it + r - 3, 1 + r)
            for q in range(PAIRS - 3, PAIRS):
                send(q, q)

        @block.scalar
        def _(act):
            sc = nc.scalar
            for dst, src in (
                (ns_col[:, :], nscale.rearrange("(d a) -> d a", a=1)),
                (w24_sb[:, :], w24), (wq_sb[:, :], wq),
                (sc_col[:, :], scale.rearrange("(a d) -> a d", a=1).to_broadcast([P, 1])),
                (bias_in[:, 0:32], b1.rearrange("(p c) -> p c", p=P)),
                (bias_in[:, 32:40], b2.rearrange("(p c) -> p c", p=P)),
                (ns_row[:, :], nscale.rearrange("(a d) -> a d", a=1).to_broadcast([P, D])),
                (gb_row[:, :], gate_b.rearrange("(a d) -> a d", a=1).to_broadcast([P, E])),
                (wout_sb[:, :], wout),
            ):
                act.dma_start(dst, src).then_inc(m["w_in"], 16)

            def deviation(h):
                act.wait_ge(m["var_ok"], h + 1)
                sc.activation(lnb[:, 3, QT * h:QT * h + QT], lnb[:, 2, QT * h:QT * h + QT], ACT.Sqrt
                              ).then_inc(m["std_ok"], 1)

            def evac_xT(g):
                act.wait_ge(m["xT_ps"], g + 1)
                if g >= 2:
                    act.wait_ge(m["kv_ps"], g - 1)
                sc.activation(xnT[:, g % 2, :], ps[:, g % 2, :], ACT.Copy).then_inc(m["xT_sb"], 1)

            def evac_q(g):
                act.wait_ge(m["q_ps"], g + 1)
                sc.activation(q_all[:, g * 512:(g + 1) * 512], ps[:, 2 + g % 2, :], ACT.Identity,
                              scale=sc_col[:, 0:1]).then_inc(m["q_sb"], 1)

            deviation(0)
            deviation(1)
            act.wait_ge(m["w_in"], 16 * N_W)
            for g in range(GROUPS):
                evac_xT(g)
                if g < 2:
                    deviation(g + 2)
                if g >= 1:
                    evac_q(g - 1)
            evac_q(GROUPS - 1)
            for i in range(4):
                act.wait_ge(m["kst_ps"], i + 1)
                sc.activation(k_stack[:, i * 1024:(i + 1) * 1024], ps[:, 6 + i % 2, :].bitcast(BF16),
                              ACT.Copy).then_inc(m["kst_sb"], 1)
            act.wait_ge(m["ms_ok"], 1)
            sc.activation(lnb[:, 5, :], lnb[:, 4, :], ACT.Sqrt).then_inc(m["rms_ok"], 1)
            act.wait_ge(m["e_ok"], 1)
            sc.activation(rs[:, 5, :], rs[:, 4, :], ACT.Exp).then_inc(m["e_exp"], 1)

            def step(u, n):
                if 0 <= n < UNITS:
                    between(u, n)
                    for k in range(CH):
                        act.wait_ge(m["exp_ps"], CH * u + k + 1)
                        if k == 0 and n >= 2:
                            act.wait_ge(m["pv_ok"], u - 1)
                        sc.activation(probs[:, n % 2, k, :], ex_bank[k % 2], ACT.Exp).then_inc(m["exp_ok"], 1)
                        if k == 2:
                            evac_s(u, n)
                        if k == 4 and n <= UNITS - 2:
                            evac_m(u, n)
                        if k == 7:
                            evac_on(u, n)
                else:
                    evac_s(u, n)
                    between(u, n)
                    if -1 <= n <= UNITS - 2:
                        evac_m(u, n)
                    evac_on(u, n)

            def between(u, n):
                if 0 <= n - 2 < UNITS:
                    act.wait_ge(m["pv_ok"], u - 1)
                    if n - 2 >= 2:
                        act.wait_ge(m["oT_ps"], u - 3)
                    sc.activation(o_T[:, n % 2, :], pv_bank[n % 2], ACT.Copy).then_inc(m["oT_sb"], 1)

            def evac_m(u, n):
                act.wait_ge(m["mT_ps"], u + 2)
                if n + 1 >= 2:
                    act.wait_ge(m_in[(n + 1) % 2], 16 * ((u + 1 - (n + 1) % 2) // 2))
                sc.activation(m_T[:, (n + 1) % 2, :], misc.bitcast(BF16)[0:3 * HU, 0:S], ACT.Copy
                              ).then_inc(m["mT_sb"], 1)

            def evac_on(u, n):
                if n % 2 == 1 and 0 <= n - 3 < UNITS:
                    act.wait_ge(m["onT_ps"], (u - 1) // 2)
                    sc.activation(o_nT[:, :], misc[:, 0:S], ACT.Copy).then_inc(m["onT_sb"], 1)

            def evac_s(u, n):
                if n % 2 == 0 and 0 <= n - 4 < UNITS:
                    act.wait_ge(m["s_ps"], (u - 2) // 2)
                    if n == 4:
                        act.wait_ge(m["route_ok"], 1)
                    sc.activation(s_all[:, bass.ds(u - 4, 2), :], misc[:, 0:2 * D].rearrange("p (t d) -> p t d", t=2),
                                  ACT.Copy).then_inc(m["s_ok"], 1)

            attention(act, step)

            act.wait_ge(m["pv_ok"], UNITS)

            def expert(q, n):
                if 0 <= n - 2 < PAIRS:
                    act.wait_ge(m["hT_ps"], q - 1)
                    if n - 2 >= 1:
                        act.wait_ge(m["y_ps"], q - 2)
                    sc.activation(hT, ps[:, 5, :], ACT.Copy, scale=0.5).then_inc(m["hT_sb"], 1)
                if 0 <= n + 1 < PAIRS:
                    act.wait_ge(m["xsT_ps"], q + 2)
                    if n + 1 >= 2:
                        act.wait_ge(m["h_ps"], q)
                    sc.activation(xT[:, (n + 1) % 2, :], ps[:, 4, 0:256], ACT.Copy).then_inc(m["xsT_sb"], 1)
                if 0 <= n < PAIRS:
                    act.wait_ge(m["g_ok"], q + 1)
                    if n >= 2:
                        act.wait_ge(m["gt_ok"], q - 1)
                    sc.activation(th[:, n % 2, :], glu[:, n % 2, :], ACT.Tanh, scale=ALPHA / 2).then_inc(m["th_ok"], 1)
                if 0 <= n - 2 < PAIRS:
                    act.wait_ge(m["y_ps"], q - 1)
                    act.wait_ge(m["p_ok"], q - 1)
                    if n - 2 >= 4:
                        act.wait_ge(y_out[(n - 2) % 4], 32 * ((q - 2 - (n - 2) % 4) // 4))
                    for t in range(2):
                        sc.activation(ys[:, (n - 2) % 4, t, :], ps[:, 6, t * D:(t + 1) * D], ACT.Identity,
                                      scale=p_st[:, (n - 2) % 4, t:t + 1]).then_inc(m["y_ok"], 1)

            experts(act, expert)

            for g in range(GROUPS):
                act.wait_ge(m["f_ok"], g + 1)
                sc.activation(fb[2 + g % 2].rearrange("p a c -> p (a c)")[:, 0:512],
                              fb[g % 2].rearrange("p a c -> p (a c)")[:, 0:512], ACT.Tanh, scale=0.5
                              ).then_inc(m["fth_ok"], 1)

        @block.tensor
        def _(pe):
            te = nc.tensor
            pe.wait_ge(m["const_in"], 3)
            pe.wait_ge(m["w24_ok"], 1)
            pe.wait_ge(m["w_in"], 16 * N_W)
            for g in range(GROUPS + 1):
                if g < GROUPS:
                    pe.wait_ge(m["xn_ok"], 4 * g + 4)
                    if g >= 2:
                        pe.wait_ge(m["xT_sb"], g - 1)
                    for t in range(4):
                        last = te.transpose(ps[:, g % 2, t * P:(t + 1) * P], xn_all[:, 4 * g + t, :], ident[:, :])
                    last.then_inc(m["xT_ps"], 1)
                if g >= 1:
                    r = (g - 1) % 2
                    pe.wait_ge(m["xT_sb"], g)
                    if g >= 3:
                        pe.wait_ge(m["q_sb"], g - 2)
                        pe.wait_ge(m["kv_sb"], g - 2)
                    te.matmul(ps[:, 2 + r, :], wq_sb[:, :], xnT[:, r, :], start=True, stop=True).then_inc(m["q_ps"], 1)
                    for t in range(4):
                        last = te.matmul(ps[:, 4 + r, t * 24:(t + 1) * 24], xnT[:, r, t * P:(t + 1) * P],
                                         w24_sb[:, :], start=True, stop=True)
                    last.then_inc(m["kv_ps"], 1)
            for i in range(4):
                pe.wait_ge(m["krow_ok"], i // 2 + 1)
                if i >= 2:
                    pe.wait_ge(m["kst_sb"], i - 1)
                for t in range(8):
                    last = te.transpose(ps[:, 6 + i % 2, :].bitcast(BF16)[:, t * P:(t + 1) * P],
                                        k_rows[:, 8 * i + t, :], ident_b[:, :])
                last.then_inc(m["kst_ps"], 1)
            pe.wait_ge(m["kv_sb"], GROUPS)
            pe.wait_ge(m["kst_sb"], 4)
            pe.wait_ge(m["q_sb"], GROUPS)
            pe.wait_ge(m["xT_sb"], GROUPS)

            def scores_exp(u, n, k):
                tt, j = k // 4, k % 4
                if k == 0:
                    pe.wait_ge(m_in[n % 2], 16 * ((u - n % 2) // 2) + 16)
                    pe.wait_ge(ke_in[(n // 2) % 2], 16 * ((u - n % 4) // 4) + 16)
                if n > 0 or k >= 2:
                    pe.wait_ge(m["exp_ok"], CH * u + k - 1)
                te.matmul(ex_bank[k % 2], k_exp[:, (n // 2) % 2, tt * P:(tt + 1) * P],
                          qs[:, n % 4, j * 512:(j + 1) * 512], start=True, stop=True).then_inc(m["exp_ps"], 1)

            def scores_max(u, n, k):
                st, j = k // 4, k % 4
                if k == 0:
                    pe.wait_ge(qs_in[n % 4], 16 * ((u - n % 4) // 4) + 16)
                    pe.wait_ge(km_in[(n // 2) % 2], 16 * ((u - n % 4) // 4) + 16)
                if n > 0 or k >= 2:
                    pe.wait_ge(m["max_ok"], CH * u + k - 1)
                for e in range(2):
                    at = (2 * j + e) * S + st * P
                    last = te.matmul(mx_bank[k % 2][:, e * S:(e + 1) * S], qs[0:MROW, n % 4, at:at + P],
                                     k_max[0:MROW, (n // 2) % 2, :], start=True, stop=True)
                last.then_inc(m["max_ps"], 1)

            def values(v, n, tt):
                if tt == 0:
                    pe.wait_ge(m["exp_ok"], CH * v + CH)
                    pe.wait_ge(v_in[(n // 2) % 2], 16 * ((v - n % 4) // 4) + 16)
                    if n >= 2:
                        pe.wait_ge(m["oT_sb"], v - 1)
                for j in range(4):
                    last = te.matmul(pv_bank[n % 2][32 * j:32 * j + 32, :], v_use[:, (n // 2) % 2, tt, :],
                                     probs[:, n % 2, 4 * tt + j, :], start=(tt == 0), stop=(tt == 1))
                if tt == 1:
                    last.then_inc(m["pv_ok"], 1)

            def turn_m(u, n):
                if not -1 <= n <= UNITS - 2:
                    return
                pe.wait_ge(m["mpart"], 5 * (u + 2))
                if n % 2 == 0 and n >= 4:
                    pe.wait_ge(m["s_ok"], (u - 2) // 2)
                elif n >= 0:
                    pe.wait_ge(m["mT_sb"], u + 1)
                for st in range(2):
                    last = te.transpose(misc.bitcast(BF16)[0:3 * HU, st * P:(st + 1) * P],
                                        m_parts[:, (n + 1) % 2, st, :, :].rearrange("p i h -> p (i h)"), ident_b[:, :])
                last.then_inc(m["mT_ps"], 1)

            def ranks():
                pe.wait_ge(m["oh_ok"], 1)
                te.matmul(oT_bank[:, 0:256], before[:, :], oh_b[:, :], start=True, stop=True)
                te.matmul(oT_bank[:, 256:512], ones_b[:, :], oh_b[:, :], start=True, stop=True
                          ).then_inc(m["rank_ps"], 1)

            def turn_o(u, n):
                if 0 <= n - 2 < UNITS:
                    pe.wait_ge(m["oT_sb"], u - 1)
                    if n - 2 == 0:
                        pe.wait_ge(m["rank_sb"], 1)
                    if n - 2 >= 1:
                        pe.wait_ge(m["on_ok"], 2 * (u - 2))
                    for i in range(4):
                        last = te.transpose(oT_bank[:, i * P:(i + 1) * P], o_T[:, n % 2, i * P:(i + 1) * P], ident[:, :])
                    last.then_inc(m["oT_ps"], 1)

            def turn_on(u, n):
                if n % 2 == 1 and 0 <= n - 3 < UNITS:
                    pe.wait_ge(m["on_ok"], 2 * (u - 1))
                    pe.wait_ge(m["mT_sb"], (u + 2) if n <= UNITS - 2 else UNITS)
                    for st in range(2):
                        last = te.transpose(misc[:, st * P:(st + 1) * P], o_n[:, st, :], ident[:, :])
                    last.then_inc(m["onT_ps"], 1)

            def project(u, n):
                if n % 2 == 0 and 0 <= n - 4 < UNITS:
                    pe.wait_ge(m["onT_sb"], (u - 2) // 2)
                    for st in range(2):
                        last = te.matmul(misc[:, st * D:(st + 1) * D], o_nT[:, st * P:(st + 1) * P], wout_sb[:, :],
                                         start=True, stop=True)
                    last.then_inc(m["s_ps"], 1)

            def step(u, n):
                for k in range(CH):
                    if 0 <= n < UNITS:
                        scores_exp(u, n, k)
                    if n + 2 < UNITS:
                        scores_max(u + 2, n + 2, k)
                    if k == 0:
                        project(u, n)
                    if k == 2:
                        turn_o(u, n)
                        if n == 1:
                            ranks()
                    if k == 3:
                        turn_m(u, n)
                        if 0 <= n - 1 < UNITS:
                            values(u - 1, n - 1, 0)
                    if k == 6:
                        turn_on(u, n)
                    if k == 7 and 0 <= n - 1 < UNITS:
                        values(u - 1, n - 1, 1)

            attention(pe, step)

            pe.wait_ge(m["s_ok"], B)
            pe.wait_ge(m["bias_r"], 16)
            pe.wait_ge(m["w1_in"], 16)
            pe.wait_ge(m["w2_in"], 16)

            packed = [None, None]

            def expert(q, n):
                if n >= 0 and n % 4 == 0:
                    for h in range(2):
                        if h == 1 or n < PAIRS:
                            packed[h] = pe.value_load(eid_i[0:1, h, bass.ds((q - n % 4) // 4, 1)],
                                                      min_val=0, max_val=8 ** 8 - 1)
                if 0 <= n - 2 < PAIRS:
                    r = n % 2
                    pe.wait_ge(m["hid_ok"], q - 1)
                    if n - 2 >= 1:
                        pe.wait_ge(m["hT_sb"], q - 2)
                    for i in range(4):
                        last = te.transpose(ps[:, 5, i * P:(i + 1) * P], hid[:, r, i * P:(i + 1) * P], ident[:, :])
                    last.then_inc(m["hT_ps"], 1)
                if 0 <= n + 1 < PAIRS:
                    pe.wait_ge(xs_in[(n + 1) % 4], 16 * ((q + 1 - (n + 1) % 4) // 4) + 16)
                    if n + 1 >= 1:
                        pe.wait_ge(m["xsT_sb"], q + 1)
                    for t in range(2):
                        last = te.transpose(ps[:, 4, t * P:(t + 1) * P], xs[:, (n + 1) % 4, t, 0:D], ident[:, :])
                    last.then_inc(m["xsT_ps"], 1)
                if 0 <= n < PAIRS:
                    if n >= 2:
                        pe.wait_ge(m["l_ok"], q - 1)
                    await_ge(pe, m["xsT_sb"], q + 1, m["pe_passed"])
                    for t in range(2):
                        e = pe.snap((packed[0] >> (3 * (2 * (n % 4) + t))) & (E - 1))
                        bank = ps[:, 2 * (n % 2) + t, :]
                        te.matmul(bank, ones_b[0:3, :], bias_rows[:, bass.ds(e * 2 * INNER, 2 * INNER)], start=True, stop=False)
                        last = te.matmul(bank, xT[:, n % 2, t * P:(t + 1) * P], w1_sb[:, bass.ds(e * 2 * INNER, 2 * INNER)],
                                         start=False, stop=True)
                    last.then_inc(m["h_ps"], 1)
                if 0 <= n - 2 < PAIRS:
                    if n - 2 >= 1:
                        pe.wait_ge(m["y_ok"], 2 * (q - 2))
                    await_ge(pe, m["hT_sb"], q - 1, m["pe_passed"])
                    for t in range(2):
                        e = pe.snap((packed[1] >> (3 * (2 * (n % 4) + t))) & (E - 1))
                        yt = ps[:, 6, t * D:(t + 1) * D]
                        te.matmul(yt, ones_b[0:3, :], bias_rows[:, bass.ds(e * D + E * 2 * INNER, D)], start=True, stop=False)
                        for c in range(2):
                            last = te.matmul(yt, hT[:, (2 * t + c) * P:(2 * t + c + 1) * P],
                                             w2_sb[:, bass.ds(e * 2 * D + c * D, D)], start=False, stop=(c == 1))
                    last.then_inc(m["y_ps"], 1)

            experts(pe, expert)

        @block.vector
        def _(dve):
            ve = nc.vector
            count = [0]

            def link(ins):
                count[0] += 1
                ins.then_inc(m["dve"], 1)
                dve.wait_ge(m["dve"], count[0])

            def statistics(h):
                dve.wait_ge(x_in[h], 16)
                for t in range(QT * h, QT * h + QT):
                    last = ve.bn_stats(st6[:, t, :], x_all[:, t, :])
                last.then_inc(m["stat"], 1)
                dve.wait_ge(m["stat"], 2 * h + 1)
                for t in range(QT * h, QT * h + QT):
                    last = ve.bn_aggr(mv[:, t, :], st6[:, t, :])
                last.then_inc(m["stat"], 1)
                dve.wait_ge(m["stat"], 2 * h + 2)
                ve.tensor_scalar(lnb[:, 2, QT * h:QT * h + QT], mv[:, QT * h:QT * h + QT, 1], EPS, None, ALU.add
                                 ).then_inc(m["var_ok"], 1)

            def norm(h):
                dve.wait_ge(m["std_ok"], h + 1)
                link(ve.reciprocal(lnb[:, 0, QT * h:QT * h + QT], lnb[:, 3, QT * h:QT * h + QT]))
                for t in range(QT * h, QT * h + QT):
                    ve.tensor_scalar(xn_all[:, t, :], x_all[:, t, :], mv[:, t, 0:1], lnb[:, 0, t:t + 1],
                                     ALU.subtract, ALU.mult).then_inc(m["xn_ok"], 1)

            def evac_kv(g):
                dve.wait_ge(m["kv_ps"], g + 1)
                ve.tensor_copy(kvg[:, 4 * g:4 * g + 4, :], ps[:, 4 + g % 2, 0:96].rearrange("p (t c) -> p t c", t=4)
                               ).then_inc(m["kv_sb"], 1)

            def key_rows(h):
                a, b = 16 * h, 16 * h + 16
                dve.wait_ge(m["kv_sb"], 4 * h + 4)
                kf = kvg[:, a:b, E:E + DK]
                link(ve.tensor_copy(k_p[:, 0, a:b, :], kf))
                link(ve.tensor_tensor(k_rest[:, 0, a:b, :], kf, k_p[:, 0, a:b, :], ALU.subtract))
                link(ve.tensor_copy(k_p[:, 1, a:b, :], k_rest[:, 0, a:b, :]))
                link(ve.tensor_tensor(k_p[:, 2, a:b, :], k_rest[:, 0, a:b, :], k_p[:, 1, a:b, :], ALU.subtract))
                for jj in range(3):
                    at = 3 * jj * DK
                    last = ve.tensor_copy(k_rows[:, a:b, at:at + 3 * DK].rearrange("p t (i d) -> p t i d", i=3),
                                          replicated(k_p[:, jj, a:b, :], 3, 2))
                last.then_inc(m["krow_ok"], 1)
                ve.tensor_copy(v_all[:, a:b, 0:DK], kvg[:, a:b, E + DK:24]).then_inc(m["v_ok"], 1)

            statistics(0)
            statistics(1)
            norm(0)
            dve.wait_ge(m["w_in"], 16 * N_W)
            ve.tensor_scalar(w24_sb[:, 0:E], w24_sb[:, 0:E], ns_col[:, 0:1], None, ALU.mult).then_inc(m["w24_ok"], 1)
            statistics(2)
            norm(1)
            evac_kv(0)
            evac_kv(1)
            statistics(3)
            norm(2)
            evac_kv(2)
            evac_kv(3)
            norm(3)
            dve.wait_ge(m["const_in"], 3)
            evac_kv(4)
            key_rows(0)
            for g in range(5, GROUPS):
                evac_kv(g)
            key_rows(1)
            link(ve.tensor_tensor(lnb[:, 6, :], mv[:, :, 1], rstd, ALU.mult))
            link(ve.tensor_tensor(lnb[:, 7, :], lnb[:, 6, :], rstd, ALU.mult))
            ve.tensor_scalar(lnb[:, 4, :], lnb[:, 7, :], EPS, None, ALU.add).then_inc(m["ms_ok"], 1)
            link(ve.tensor_copy(bias_parts[:, 0, :], bias_in[:, :]))
            link(ve.tensor_tensor(bias_rest[:, 0, :], bias_in[:, :], bias_parts[:, 0, :], ALU.subtract))
            link(ve.tensor_copy(bias_parts[:, 1, :], bias_rest[:, 0, :]))
            ve.tensor_tensor(bias_parts[:, 2, :], bias_rest[:, 0, :], bias_parts[:, 1, :], ALU.subtract).then_inc(m["bias_ok"], 1)

            def t3(i):
                return rt[:, i, :].rearrange("p (t e) -> p t e", e=E)

            def over_e(col):
                return replicated(col, E, 2)

            def over_t(row):
                return replicated(row, TILES, 1)


            def best_two():
                dve.wait_ge(m["rms_ok"], 1)
                link(ve.reciprocal(rms, lnb[:, 5, :]))
                yield
                link(ve.tensor_tensor(t3(0), kvg[:, :, 0:E], over_e(rms), ALU.mult))
                yield
                link(ve.tensor_tensor(t3(1), t3(0), over_t(gb_row[:, :]), ALU.add))
                yield
                link(ve.tensor_reduce(rs[:, 0, :], t3(1), AX, ALU.max))
                yield
                link(ve.tensor_tensor(t3(2), t3(1), over_e(rs[:, 0, :]), ALU.is_equal))
                yield
                link(ve.tensor_tensor(t3(3), t3(2), over_t(rev8[:, :]), ALU.mult))
                yield
                link(ve.tensor_reduce(rs[:, 1, :], t3(3), AX, ALU.max))
                yield
                link(ve.tensor_tensor(t3(4), t3(3), over_e(rs[:, 1, :]), ALU.is_equal))
                yield
                link(ve.scalar_tensor_tensor(t3(5), t3(4), -BIG, t3(1), ALU.mult, ALU.add))
                yield
                link(ve.tensor_reduce(rs[:, 2, :], t3(5), AX, ALU.max))
                yield
                ve.tensor_tensor(rs[:, 4, :], rs[:, 2, :], rs[:, 0, :], ALU.subtract).then_inc(m["e_ok"], 1)
                link(ve.tensor_tensor(t3(6), t3(5), over_e(rs[:, 2, :]), ALU.is_equal))
                yield
                link(ve.tensor_tensor(t3(7), t3(6), over_t(rev8[:, :]), ALU.mult))
                yield
                link(ve.tensor_reduce(rs[:, 3, :], t3(7), AX, ALU.max))
                yield
                link(ve.tensor_tensor(t3(8), t3(7), over_e(rs[:, 3, :]), ALU.is_equal))
                yield
                ve.tensor_tensor(oh_b[:, :], rt[:, 4, :], rt[:, 8, :], ALU.add).then_inc(m["oh_ok"], 1)
                dve.wait_ge(m["e_exp"], 1)
                link(ve.tensor_scalar(rs[:, 6, :], rs[:, 5, :], 1.0, None, ALU.add))
                yield
                link(ve.reciprocal(rs[:, 7, :], rs[:, 6, :]))
                yield
                ve.tensor_copy(meta[:, :, 0, 1], rs[:, 7, :])
                ve.tensor_tensor(meta[:, :, 1, 1], rs[:, 7, :], rs[:, 5, :], ALU.mult)

            def sorted_places():
                pad = 16 * E
                tot = t3(0)
                rank = t3(1)
                dve.wait_ge(m["rank_ps"], 1)
                ve.tensor_copy(rt[:, 1, :], oT_bank[:, 0:256])
                ve.tensor_copy(rt[:, 0, :], oT_bank[:, 256:512]).then_inc(m["rank_sb"], 1)
                dve.wait_ge(m["rank_sb"], 1)
                link(ve.tensor_copy(scan[:, 0, pad:], tot.rearrange("p t e -> p (t e)")))
                yield
                src = 0
                for d in (1, 2, 4, 8, 16):
                    link(ve.tensor_tensor(scan[:, 1 - src, pad:], scan[:, src, pad:],
                                          scan[:, src, pad - d * E:pad - d * E + TILES * E], ALU.add))
                    yield
                    src = 1 - src
                incl = scan[:, src, pad:].rearrange("p (t e) -> p t e", e=E)
                counts = scan[:, src, pad + (TILES - 1) * E:]
                link(ve.tensor_tensor(t3(9), incl, tot, ALU.subtract))
                yield
                link(ve.tensor_tensor(t3(10), t3(9), rank, ALU.add))
                yield
                link(ve.memset(nt[:, :, :], 0.0))
                yield
                link(ve.tensor_tensor(cmp_n[:, :, :], replicated(counts, TILES, 2), replicated(steps128[:, :], E, 1), ALU.is_gt))
                yield
                link(ve.tensor_reduce(nt[:, 0, 8:16], cmp_n[:, :, :], AX, ALU.add))
                yield
                for i, d in enumerate((1, 2, 4)):
                    link(ve.tensor_tensor(nt[:, i + 1, 8:16], nt[:, i, 8:16], nt[:, i, 8 - d:16 - d], ALU.add))
                    yield
                link(ve.tensor_tensor(nt[:, 4, 8:16], nt[:, 3, 8:16], nt[:, 0, 8:16], ALU.subtract))
                yield
                link(ve.tensor_scalar(nt[:, 5, 8:16], nt[:, 4, 8:16], float(P), None, ALU.mult))
                yield
                link(ve.tensor_tensor(t3(11), t3(10), over_t(nt[:, 5, 8:16]), ALU.add))
                yield
                for k, oh in enumerate((4, 8)):
                    link(ve.tensor_tensor(t3(9), t3(oh), t3(11), ALU.mult))
                    yield
                    link(ve.tensor_reduce(rs[:, 8 + k, :], t3(9), AX, ALU.add))
                    yield
                    ve.tensor_copy(pos_i[:, :, k], rs[:, 8 + k, :])
                link(ve.tensor_tensor(cmp_t[:, :, :], replicated(tile_no[:, :], E, 2),
                                      replicated(nt[:, 3, 8:16], SORTED, 1), ALU.is_ge))
                yield
                link(ve.tensor_reduce(cmp_s[:, :], cmp_t[:, :, :], AX, ALU.add))
                yield
                link(ve.tensor_scalar(eid_f[:, 4:4 + SORTED], cmp_s[:, :], float(E - 1), None, ALU.min))
                yield
                for h, at in enumerate((4, 0)):
                    tiles8 = eid_f[:, at:at + 80].rearrange("p (i j) -> p i j", j=8)
                    link(ve.tensor_tensor(eid_p[:, :, :], tiles8, replicated(pow8[:, :], 10, 1), ALU.mult))
                    yield
                    link(ve.tensor_reduce(eid_s[:, h, :], eid_p[:, :, :], AX, ALU.add))
                    yield
                ve.tensor_copy(eid_i[:, :, :], eid_s[0:1, :, :]).then_inc(m["route_ok"], 1)


            routing = [best_two(), sorted_places()]

            def route(n, k):
                if n < 1:
                    next(routing[0], None)
                elif n > 1 or k >= 4:
                    next(routing[1], None)

            def normalise(u, n):
                if not 0 <= n - 2 < UNITS:
                    return
                c = n % 2
                ov = oT_bank.rearrange("p (e t j d) -> p e t j d", e=2, t=2, j=4)
                dve.wait_ge(m["oT_ps"], u - 1)
                if n >= 3:
                    dve.wait_ge(m["on_ok"], 2 * (u - 2))
                ve.reciprocal(inv_sum[:, c, :, :], oT_bank.rearrange("p (i j d) -> p i j d", i=4, j=4)[:, :, :, DK]
                              ).then_inc(m["inv_ok"], 1)
                dve.wait_ge(m["inv_ok"], u - 1)
                if c == 0 and n >= 4:
                    dve.wait_ge(m["onT_ps"], (u - 2) // 2)
                for st in range(2):
                    dst = o_n[:, st, :].rearrange("p (c j e d) -> p c e j d", c=2, j=4, e=2)[:, c, :, :, :]
                    inv = inv_sum[:, c, :, :].rearrange("p (e t) j -> p e t j", e=2)[:, :, st, :]
                    ve.tensor_tensor(dst, ov[:, :, st, :, 0:DK], replicated(inv, DK, 3), ALU.mult
                                     ).then_inc(m["on_ok"], 1)

            def split_m(u, n):
                r = n % 2
                mx = maxes[:, r, :, :]
                dve.wait_ge(m["max_ok"], CH * u + CH)
                if n >= 2:
                    dve.wait_ge(m["mT_ps"], u - 1)
                ve.tensor_scalar(m_parts[:, r, :, 0, :], mx, -1.0, None, ALU.mult).then_inc(m["mpart"], 1)
                dve.wait_ge(m["mpart"], 5 * u + 1)
                ve.tensor_tensor(m_rest[:, r, 0, :, :], mx, m_parts[:, r, :, 0, :], ALU.add).then_inc(m["mpart"], 1)
                dve.wait_ge(m["mpart"], 5 * u + 2)
                ve.tensor_scalar(m_parts[:, r, :, 1, :], m_rest[:, r, 0, :, :], -1.0, None, ALU.mult).then_inc(m["mpart"], 1)
                dve.wait_ge(m["mpart"], 5 * u + 3)
                ve.tensor_tensor(m_rest[:, r, 1, :, :], m_rest[:, r, 0, :, :], m_parts[:, r, :, 1, :], ALU.add).then_inc(m["mpart"], 1)
                dve.wait_ge(m["mpart"], 5 * u + 4)
                ve.tensor_scalar(m_parts[:, r, :, 2, :], m_rest[:, r, 1, :, :], -1.0, None, ALU.mult).then_inc(m["mpart"], 1)

            def step(u, n):
                if n + 2 < UNITS:
                    for k in range(CH):
                        st, j = k // 4, k % 4
                        dve.wait_ge(m["max_ps"], CH * (u + 2) + k + 1)
                        ve.tensor_reduce(maxes[:, n % 2, st, 2 * j:2 * j + 2],
                                         mx_bank[k % 2].rearrange("p (e t) -> p e t", e=2), AX, ALU.max
                                         ).then_inc(m["max_ok"], 1)
                        if n < 4:
                            route(n, k)
                        if k == 4:
                            normalise(u, n)
                    split_m(u + 2, n + 2)
                    if n == 3:
                        for _ in routing[1]:
                            pass
                else:
                    normalise(u, n)

            attention(dve, step)
            dve.wait_ge(m["pv_ok"], UNITS)

            def expert(q, n):
                if not 0 <= n < PAIRS:
                    return
                r = n % 2
                hb = ps[:, 2 * r:2 * r + 2, :]
                g3 = glu[:, r, :].rearrange("p (t c) -> p t c", t=2)
                l3 = lin[:, r, :].rearrange("p (t c) -> p t c", t=2)
                dve.wait_ge(m["h_ps"], q + 1)
                if n >= 2:
                    dve.wait_ge(m["gt_ok"], q - 1)
                    dve.wait_ge(m["hid_ok"], q - 1)
                ve.tensor_scalar(g3, hb[:, :, 0:INNER], LIMIT, None, ALU.min).then_inc(m["g_ok"], 1)
                ve.tensor_scalar(l3, hb[:, :, INNER:], LIMIT, -LIMIT, ALU.min, ALU.max).then_inc(m["l_ok"], 1)
                dve.wait_ge(m["g_ok"], q + 1)
                dve.wait_ge(m["th_ok"], q + 1)
                ve.scalar_tensor_tensor(gt[:, r, :], th[:, r, :], 1.0, glu[:, r, :], ALU.add, ALU.mult).then_inc(m["gt_ok"], 1)
                dve.wait_ge(m["gt_ok"], q + 1)
                dve.wait_ge(m["l_ok"], q + 1)
                if n >= 2:
                    dve.wait_ge(m["hT_ps"], q - 1)
                ve.scalar_tensor_tensor(hid[:, r, :], lin[:, r, :], 1.0, gt[:, r, :], ALU.add, ALU.mult).then_inc(m["hid_ok"], 1)

            experts(dve, expert)

            fin = [0]

            def linkf(ins):
                fin[0] += 1
                ins.then_inc(m["dve"], 1)
                dve.wait_ge(m["dve"], count[0] + fin[0])

            def add_up(g):
                f = fb[g % 2].rearrange("p a c -> p (a c)")[:, 0:512].rearrange("p (t d) -> p t d", t=4)
                dve.wait_ge(yb_in[g % 4], 16 * (g // 4) + 16)
                if g >= 2:
                    dve.wait_ge(m["o_ok"], g - 1)
                linkf(ve.tensor_tensor(f, xn_all[:, 4 * g:4 * g + 4, :], yb[:, g % 4, :, 0:D], ALU.add))
                ve.tensor_tensor(f, f, yb[:, g % 4, :, D:2 * D], ALU.add).then_inc(m["f_ok"], 1)

            add_up(0)
            for g in range(GROUPS):
                if g + 1 < GROUPS:
                    add_up(g + 1)
                f = fb[g % 2].rearrange("p a c -> p (a c)")[:, 0:512].rearrange("p (t d) -> p t d", t=4)
                tf = fb[2 + g % 2].rearrange("p a c -> p (a c)")[:, 0:512].rearrange("p (t d) -> p t d", t=4)
                xg = x_all[:, 4 * g:4 * g + 4, :]
                dve.wait_ge(m["f_ok"], g + 1)
                dve.wait_ge(m["fth_ok"], g + 1)
                linkf(ve.scalar_tensor_tensor(f, tf, 1.0, f, ALU.add, ALU.mult))
                linkf(ve.scalar_tensor_tensor(f, f, 0.5, s_all[:, 4 * g:4 * g + 4, :], ALU.mult, ALU.mult))
                ve.tensor_tensor(xg, xg, f, ALU.add).then_inc(m["o_ok"], 1)


def kernel(L0_attn_x, L0_attn_w_q, L0_attn_w_k, L0_attn_w_v, L0_attn_w_out, L0_attn_softmax_scale,
           L0_ffn_norm_scale, L0_ffn_gate_w, L0_ffn_gate_b, L0_ffn_mlp1_w, L0_ffn_mlp1_b, L0_ffn_mlp2_w,
           L0_ffn_mlp2_b):
    import concourse.bacc as bacc
    from concourse.bass_utils import run_bass_kernel_spmd

    order = [4 * j + 2 * c + e for c in range(2) for j in range(4) for e in range(2)]
    a = {}
    a["x"] = np.ascontiguousarray(L0_attn_x).reshape(TOKENS, D)
    wq = np.asarray(L0_attn_w_q).reshape(HEADS, DK, D)[order]
    a["wq"] = np.ascontiguousarray(wq.transpose(2, 1, 0).reshape(D, D))
    a["w24"] = np.ascontiguousarray(np.concatenate(
        [np.asarray(L0_ffn_gate_w), np.asarray(L0_attn_w_k).T, np.asarray(L0_attn_w_v).T], axis=1))
    wo = np.asarray(L0_attn_w_out).reshape(D, HEADS, DK)[:, order]
    a["wout"] = np.ascontiguousarray(wo.reshape(D, D).T)
    a["nscale"] = np.ascontiguousarray(L0_ffn_norm_scale)
    a["gate_b"] = np.ascontiguousarray(L0_ffn_gate_b)
    w1 = np.asarray(L0_ffn_mlp1_w).reshape(E, D, INNER, 2)
    a["w1"] = np.ascontiguousarray(w1.transpose(1, 0, 3, 2).reshape(D, E * 2 * INNER))
    a["b1"] = np.ascontiguousarray(np.asarray(L0_ffn_mlp1_b).reshape(E, INNER, 2).transpose(0, 2, 1).reshape(-1))
    w2 = np.asarray(L0_ffn_mlp2_w).reshape(E, 2, P, D)
    a["w2"] = np.ascontiguousarray(w2.transpose(2, 0, 1, 3).reshape(P, E * 2 * D))
    a["b2"] = np.ascontiguousarray(L0_ffn_mlp2_b).reshape(-1)
    a["scale"] = np.ascontiguousarray(L0_attn_softmax_scale)

    nc = bacc.Bacc("TRN2", target_bir_lowering=False, num_devices=1)
    arrays = {f"in_{k}": v for k, v in a.items()}
    args = [nc.dram_tensor(k, v.shape, mybir.dt.from_np(v.dtype), kind="ExternalInput").ap() for k, v in arrays.items()]
    out = nc.dram_tensor("out_0", (TOKENS, D), F32, kind="ExternalOutput").ap()
    build(nc, *args, out)
    res = run_bass_kernel_spmd(nc, [arrays], core_ids=[0])
    return res.results[0]["out_0"].reshape(B, S, D)
```

```python
from contextlib import ExitStack

import numpy as np
import concourse.bass as bass
from concourse import mybir
from concourse.alu_op_type import AluOpType as ALU

ACT = mybir.ActivationFunctionType
F32 = mybir.dt.float32
BF16 = mybir.dt.bfloat16
I32 = mybir.dt.int32
AX = mybir.AxisListType.X

P = 128
B, S, D = 16, 256, 128
HEADS = 16
DK = D // HEADS
TOKENS = B * S
TILES = TOKENS // P
GROUPS = TILES // 4
E, INNER, TOPK = 8, 256, 2
LIMIT, ALPHA, EPS = 7.0, 1.702, 1e-5
UNITS = 2 * B
HU = HEADS // 2
UCOLS = HU * S
CH = 8
KROWS = 9 * DK
MROW = 96
SORTED = TOPK * TOKENS // P + E
PAIRS = SORTED // 2
ROW = D + 4
BIG = 3.0e38


def replicated(ap, times, at):
    dims = [list(d) for d in ap.ap]
    return bass.AP(ap.tensor, ap.offset, dims[:at] + [[0, times]] + dims[at:])


def await_ge(eng, semaphore, value, passed):
    eng.wait_ge(semaphore, value)
    if not isinstance(value, int):
        eng.sem_inc(passed, 1)


def build(nc, x, wq, w24, wout, nscale, gate_b, w1, b1, w2, b2, scale, out):
    ctx = ExitStack()
    with ctx:
        def sb(name, shape, dt=F32):
            return ctx.enter_context(nc.sbuf_tensor(name, shape, dt))

        def sem(name):
            return ctx.enter_context(nc.semaphore(name))

        q_dram = nc.dram_tensor("q_dram", [B, 3, P, S], BF16, kind="Internal").ap()
        bias_dram = nc.dram_tensor("bias_dram", [3, E * 2 * INNER + E * D], BF16, kind="Internal").ap()
        sorted_dram = nc.dram_tensor("sorted_dram", [SORTED * P, ROW], F32, kind="Internal").ap()
        y_dram = nc.dram_tensor("y_dram", [TOPK * TOKENS + SORTED * P, D], F32, kind="Internal").ap()

        x_all = sb("x_all", [P, TILES, D])
        xn_all = sb("xn_all", [P, TILES, D])
        s_all = sb("s_all", [P, TILES, D])
        w1_sb = sb("w1_sb", [P, E * 2 * INNER])
        w2_sb = sb("w2_sb", [P, E * 2 * D])
        bias_rows = sb("bias_rows", [3, E * 2 * INNER + E * D], BF16)
        wq_sb = sb("wq_sb", [P, D])
        wout_sb = sb("wout_sb", [P, D])
        w24_sb = sb("w24_sb", [P, 24])
        ns_col = sb("ns_col", [P, 1])
        ns_row = sb("ns_row", [P, D])
        gb_row = sb("gb_row", [P, E])
        sc_col = sb("sc_col", [P, 1])
        bias_in = sb("bias_in", [P, 40])
        bias_rest = sb("bias_rest", [P, 2, 40])
        bias_parts = sb("bias_parts", [P, 3, 40], BF16)
        ident = sb("ident", [P, P])
        ident_b = sb("ident_b", [P, P], BF16)
        before = sb("before", [P, P], BF16)
        ones_b = sb("ones_b", [P, P], BF16)
        ones_f = sb("ones_f", [P, P])
        rev8 = sb("rev8", [P, E])
        steps128 = sb("steps128", [P, TILES])
        tile_no = sb("tile_no", [P, SORTED])
        meta = sb("meta", [P, TILES, TOPK, 2])
        pad_row = sb("pad_row", [P, ROW])
        root1 = sb("root1", [P, 1])
        st6 = sb("st6", [P, TILES, 6])
        mv = sb("mv", [P, TILES, 2])
        lnb = sb("lnb", [P, 8, TILES])
        rstd, rms = lnb[:, 0, :], lnb[:, 1, :]
        xnT = sb("xnT", [P, 2, 512])
        q_all = sb("q_all", [P, TOKENS])
        q_parts = sb("q_parts", [P, 2, 3, 512], BF16)
        q_rest = sb("q_rest", [P, 2, 512])
        kvg = sb("kvg", [P, TILES, 24])
        k_p = sb("k_p", [P, 3, TILES, DK], BF16)
        k_stack = sb("k_stack", [P, TOKENS], BF16)
        v_all = sb("v_all", [P, TILES, 32])
        qs = sb("qs", [P, 4, UCOLS], BF16)
        k_max = sb("k_max", [P, 2, S], BF16)
        k_exp = sb("k_exp", [P, 2, S], BF16)
        v_use = sb("v_use", [P, 2, 2, 32])
        probs = sb("probs", [P, 2, CH, 512])
        maxes = sb("maxes", [P, 2, 2, HU])
        m_rest = sb("m_rest", [P, 2, 2, 2, HU])
        m_parts = sb("m_parts", [P, 2, 2, 3, HU], BF16)
        m_T = sb("m_T", [3 * HU, 2, S], BF16)
        o_T = sb("o_T", [P, 2, 512])
        inv_sum = sb("inv_sum", [P, 2, 4, 4])
        o_n = sb("o_n", [P, 2, D])
        o_nT = sb("o_nT", [P, S])
        rs = sb("rs", [P, 10, TILES])
        oh_b = sb("oh_b", [P, TILES * E], BF16)
        nt = sb("nt", [P, 6, 16])
        pos_i = sb("pos_i", [P, TILES, TOPK], I32)
        eid_f = sb("eid_f", [P, SORTED + 16])
        pow8 = sb("pow8", [P, 8])
        eid_p = sb("eid_p", [P, 10, 8])
        eid_s = sb("eid_s", [P, 2, 10])
        eid_i = sb("eid_i", [1, 2, 10], I32)
        pf = probs[:, :, :, :].rearrange("p a b c -> p (a b c)")
        rt = s_all[:, 8:TILES, :].rearrange("p (i t) d -> p i (t d)", t=2)
        scan = w1_sb[:, 0:768].rearrange("p (i c) -> p i c", i=2)
        cmp_n = w1_sb[:, 768:1024].rearrange("p (e t) -> p e t", e=E)
        cmp_t = w1_sb[:, 1024:1600].rearrange("p (t e) -> p t e", e=E)
        cmp_s = w1_sb[:, 1600:1672]
        k_rest = pf[:, 4672:5184].rearrange("p (i t d) -> p i t d", i=2, d=DK)
        k_rows = pf[:, 5184:7232].bitcast(BF16).rearrange("p (t c) -> p t c", c=P)
        t_raw = sb("t_raw", [P, 2, D])
        r_col = sb("r_col", [P, 2, 1])
        pos_st = sb("pos_st", [P, 2, TOPK], I32)
        row_st = sb("row_st", [P, 2, TOPK, ROW])
        xs = sb("xs", [P, 4, 2, ROW])
        xT = pf[:, 0:512].rearrange("p (a c) -> p a c", a=2)
        glu = pf[:, 512:1536].rearrange("p (a c) -> p a c", a=2)
        lin = pf[:, 1536:2560].rearrange("p (a c) -> p a c", a=2)
        th = pf[:, 2560:3584].rearrange("p (a c) -> p a c", a=2)
        gt = pf[:, 3584:4608].rearrange("p (a c) -> p a c", a=2)
        hid = pf[:, 4608:5632].rearrange("p (a c) -> p a c", a=2)
        hT = pf[:, 5632:6144]
        ys = pf[:, 6144:7168].rearrange("p (a t c) -> p a t c", a=4, t=2)
        pad_at = sb("pad_at", [P, 4, 2])
        p_st = sb("p_st", [P, 4, 2])
        dest_i = sb("dest_i", [P, 4, 2], I32)
        yb = q_all[:, :].rearrange("p (a t c) -> p a t c", a=4, t=4)
        fb = qs[:, :, :].rearrange("p i c -> p (i c)").bitcast(F32).rearrange("p (a t d) -> p a t d", a=8, t=4)

        ps = ctx.enter_context(nc.psum_tensor("ps", [P, 8, 512], F32))
        ex_bank = [ps[:, 0, :], ps[:, 1, :], ps[:, 5, :]]
        mx_bank = [ps[:, 2, :], ps[:, 3, :], ps[:, 6, :]]
        BANKS = ((0, 1, 2, 0, 1, 2, 0, 1), (2, 0, 1, 2, 0, 1, 2, 1))
        pv_bank = ps[:, 4, :]
        key_bank = [ps[:, 6, :], ps[:, 7, :], pv_bank, ex_bank[2]]
        onT_ps, s_ps = ps[:, 7, 0:S], ps[:, 7, 0:2 * D]
        mT_ps = ps[:, 7, S:S + S // 2].bitcast(BF16)[0:3 * HU, :]

        names = """x_in0 x_in1 x_in2 x_in3 wp_in w_in w2_in w1_in w24_ok pad_in ident_ok krow_in const_in stat var_ok std_ok ms_ok rms_ok xn_ok xT_ps xT_sb q_ps q_sb kv_ps kv_sb
            krow_ok kst_ps kst_sb v_ok bias_ok bias_w bias_r dve ones_in
            qpart q_w0 q_w1 qs_in0 qs_in1 qs_in2 qs_in3 km_in0 km_in1 ke_in0 ke_in1 v_in0 v_in1
            max_ps max_ok mpart mT_ps mT_sb m_in0 m_in1 exp_ps exp_ok pv_ok oT_sb oT_ps inv_ok on_ok onT_ps onT_sb
            s_ps s_ok oh_ok rank_ps rank_sb e_ok e_exp route_ok prow pool_row scat0 scat1
            xs_in0 xs_in1 xs_in2 xs_in3 xsT_ps xsT_sb h_ps g_ok l_ok th_ok gt_ok hid_ok hT_ps hT_sb y_ps y_ok dest_ok p_ok y_out0 y_out1 y_out2 y_out3
            yb_in0 yb_in1 yb_in2 yb_in3 f_ok fth_ok fy_ok fp_ok silu_ok so_ok o_ok out_done pool_passed sp_passed pe_passed""".split()
        m = {n: sem(n) for n in names}
        q_w = [m["q_w0"], m["q_w1"]]
        qs_in = [m[f"qs_in{i}"] for i in range(4)]
        km_in, ke_in, v_in = ([m[f"{n}_in{i}"] for i in range(2)] for n in ("km", "ke", "v"))
        m_in = [m["m_in0"], m["m_in1"]]
        xs_in = [m[f"xs_in{i}"] for i in range(4)]
        yb_in = [m[f"yb_in{i}"] for i in range(4)]
        scat = [m["scat0"], m["scat1"]]
        y_out = [m[f"y_out{i}"] for i in range(4)]
        x_in = [m[f"x_in{i}"] for i in range(4)]
        N_WP, N_W = 4, 5
        TURN_O_AT, PROJECT_AT, TURN_M_AT, TURN_ON_AT, VALUES_AT = 1, 1, 4, 7, (6, 7)
        EVAC_S_AT, EVAC_M_AT, EVAC_ON_AT = 2, 3, 7
        HALF_AT = 2
        NORM_AT = 2
        QT = TILES // 4

        def on_pool(g):
            return g in (2, 4, 6)

        def f_of(g):
            return fb[:, g % 4, :, :]

        def attention(eng, step):
            for u in range(-2, 4):
                step(u, u)
            with eng.Fori(1, UNITS // 4 - 1) as it:
                for r in range(4):
                    step(4 * it + r, 4 + r)
            for u in range(UNITS - 4, UNITS):
                step(u, u)

        def last_and_first(attend, expert):
            for i in range(3):
                attend(UNITS + i, UNITS + i)
                expert(i - 1, i - 1)

        def experts(eng, step):
            for q in range(2, 8):
                step(q, q)
            with eng.Fori(2, PAIRS // 4 - 1) as it:
                for r in range(4):
                    step(4 * it + r, 8 + r)
            for q in range(PAIRS - 4, PAIRS + 2):
                step(q, q)

        block = ctx.enter_context(nc.Block())

        @block.sync
        def _(sp):
            xv = x.rearrange("(t p) d -> p t d", p=P)
            for h in range(4):
                sp.dma_start(x_all[:, QT * h:QT * h + QT, :], xv[:, QT * h:QT * h + QT, :]).then_inc(x_in[h], 16)
            for dst, src in (
                (bias_in[:, 0:32], b1.rearrange("(p c) -> p c", p=P)),
                (bias_in[:, 32:40], b2.rearrange("(p c) -> p c", p=P)),
                (ns_row[:, :], nscale.rearrange("(a d) -> a d", a=1).to_broadcast([P, D])),
                (gb_row[:, :], gate_b.rearrange("(a d) -> a d", a=1).to_broadcast([P, E])),
                (wout_sb[:, :], wout),
            ):
                sp.dma_start(dst, src).then_inc(m["w_in"], 16)
            def load_q(u, n, g, gn):
                await_ge(sp, q_w[gn % 2], 32 * (g // 2) + 32, m["sp_passed"])
                if n >= 4:
                    await_ge(sp, m["exp_ps"], CH * (u - 3), m["sp_passed"])
                src = q_dram[bass.ds(2 * g + (n % 4) // 2, 1)].rearrange("a i (d h) s -> (a i d) (h s)", d=DK)
                src = src[:, (n % 2) * UCOLS:(n % 2 + 1) * UCOLS]
                sp.dma_start(qs[0:KROWS, n % 4, :], replicated(src, 3, 0)).then_inc(qs_in[n % 4], 16)

            def load_k(dst, b, s):
                sp.dma_start(dst, k_stack[:, bass.ds(b * S, S)]).then_inc(s, 16)

            def load_v(b, n):
                sp.dma_start(v_use[:, n % 2, :, :], v_all[:, bass.ds(2 * b, 2), :]).then_inc(v_in[n % 2], 16)

            await_ge(sp, m["ones_in"], 1, m["sp_passed"])
            for u in range(3):
                load_q(u, u, 0, 0)
            await_ge(sp, m["kst_sb"], 1, m["sp_passed"])
            await_ge(sp, m["v_ok"], 1, m["sp_passed"])
            load_k(k_max[:, 0, :], 0, km_in[0])
            load_k(k_max[:, 1, :], 1, km_in[1])
            load_k(k_exp[:, 0, :], 0, ke_in[0])
            load_v(0, 0)
            def load_early(n):
                if n < 4:
                    if n == 0:
                        sp.wait_ge(m["const_in"], 1)
                    at = n * SORTED // 4
                    sp.dma_start(sorted_dram.rearrange("(t p) c -> p t c", p=P)[:, at:at + SORTED // 4, :],
                                 replicated(pad_row[:, :], SORTED // 4, 1)).then_inc(m["pad_in"], 16)
                else:
                    if n == 4:
                        sp.dma_start(w2_sb[:, :], w2).then_inc(m["w2_in"], 16)
                        sp.wait_ge(m["route_ok"], 1)
                    at = (n - 4) * E * 2 * INNER // 4
                    sp.dma_start(w1_sb[:, at:at + E * 2 * INNER // 4], w1[:, at:at + E * 2 * INNER // 4]
                                 ).then_inc(m["w1_in"], 16)

            def turn(u, n):
                if n >= 0:
                    loads(u, n)
                if -1 <= n <= UNITS - 2:
                    await_ge(sp, m["mT_sb"], u + 2, m["sp_passed"])
                    sp.dma_start(qs[MROW:MROW + 3, (n + 1) % 4, :], m_T[:, (n + 1) % 2, :]
                                 ).then_inc(m_in[(n + 1) % 2], 16)

            def loads(u, n):
                if n + 3 < UNITS:
                    load_q(u + 3, n + 3, (u - n % 4) // 4 + (n % 4 + 3) // 4, n // 4 + (n % 4 + 3) // 4)
                if n % 2 == 0 and n // 2 + 2 < B:
                    await_ge(sp, m["max_ps"], CH * (u + 2), m["sp_passed"])
                    if n < 4:
                        sp.wait_ge(m["kst_sb"], 4)
                    load_k(k_max[:, (n // 2) % 2, :], (u - n % 2) // 2 + 2, km_in[(n // 2) % 2])
                if n % 2 == 0 and n // 2 + 1 < B:
                    if n >= 2:
                        await_ge(sp, m["exp_ps"], CH * u, m["sp_passed"])
                    load_k(k_exp[:, (n // 2 + 1) % 2, :], (u - n % 2) // 2 + 1, ke_in[(n // 2 + 1) % 2])
                if n % 2 == 1 and n // 2 + 1 < B:
                    if n >= 3:
                        await_ge(sp, m["pv_ok"], u - 1, m["sp_passed"])
                    else:
                        sp.wait_ge(m["v_ok"], 2)
                    load_v((u - 1) // 2 + 1, n // 2 + 1)

            for u in range(-1, 8):
                turn(u, u)
                if u >= 0:
                    load_early(u)
                if u == -1:
                    sp.wait_ge(m["bias_ok"], 1)
                    n1 = E * 2 * INNER
                    sp.dma_start(bias_dram[:, 0:n1].rearrange("i (p c) -> p i c", p=P),
                                 bias_parts[:, :, 0:32]).then_inc(m["bias_w"], 16)
                    sp.dma_start(bias_dram[:, n1:].rearrange("i (p c) -> p i c", p=P),
                                 bias_parts[:, :, 32:40]).then_inc(m["bias_w"], 16)
                if u == 3:
                    sp.wait_ge(m["bias_w"], 32)
                    sp.dma_start(bias_rows[:, :], bias_dram).then_inc(m["bias_r"], 16)
            with sp.Fori(1, 3) as it:
                for r in range(8):
                    turn(8 * it + r, 8 + r)
            for u in range(24, UNITS):
                turn(u, u)

            await_ge(sp, scat[0], 8 * TOPK * TILES, m["sp_passed"])
            await_ge(sp, scat[1], 8 * TOPK * TILES, m["sp_passed"])

            def load_sorted(q, n):
                if n >= 4:
                    await_ge(sp, m["xsT_ps"], q - 3, m["sp_passed"])
                    await_ge(sp, m["p_ok"], q - 3, m["sp_passed"])
                    await_ge(sp, m["dest_ok"], 3 * (q - 3), m["sp_passed"])
                sp.dma_start(xs[:, n % 4, :, :],
                             sorted_dram[bass.ds(q * 2 * P, 2 * P), :].rearrange("(t p) c -> p t c", p=P)
                             ).then_inc(xs_in[n % 4], 16)

            for q in range(4):
                load_sorted(q, q)
            with sp.Fori(1, PAIRS // 4) as it:
                for r in range(4):
                    load_sorted(4 * it + r, 4 + r)

            for r in range(4):
                await_ge(sp, y_out[r], 4 * SORTED, m["sp_passed"])
            yv = y_dram[0:TOPK * TOKENS, :].rearrange("(t p k) d -> p t (k d)", p=P, k=TOPK)
            ov = out.rearrange("(t p) d -> p t d", p=P)
            for g in range(4):
                sp.dma_start(yb[:, g, :, :], yv[:, 4 * g:4 * g + 4, :]).then_inc(yb_in[g], 16)
            for g in range(GROUPS):
                if g + 4 < GROUPS:
                    sp.wait_ge(m["f_ok"], g + 1)
                    sp.dma_start(yb[:, g, :, :], yv[:, 4 * g + 16:4 * g + 20, :]).then_inc(yb_in[g], 16)
                sp.wait_ge(m["o_ok"], g + 1)
                sp.dma_start(ov[:, 4 * g:4 * g + 4, :], x_all[:, 4 * g:4 * g + 4, :]).then_inc(m["out_done"], 16)
            await_ge(sp, m["out_done"], 16 * GROUPS, m["sp_passed"])

        @block.gpsimd
        def _(pool):
            gp = nc.gpsimd
            count = [0]

            def link(ins):
                count[0] += 1
                ins.then_inc(m["prow"], 1)
                await_ge(pool, m["prow"], count[0], m["pool_passed"])

            link(gp.memset(ones_f[:, :], 1.0))
            link(gp.affine_select(out=ident[:, :], in_=ones_f[:, :], compare_op=ALU.is_equal, fill=0.0, base=0,
                                  pattern=[[-1, P]], channel_multiplier=1))
            gp.tensor_copy(ident_b[:, :], ident[:, :]).then_inc(m["ident_ok"], 1)
            link(gp.memset(k_rows[:, :, KROWS:P], 0.0))
            gp.memset(k_rows[:, :, MROW:MROW + 3], 1.0).then_inc(m["krow_in"], 1)
            link(gp.memset(v_all[:, :, :], 0.0))
            gp.memset(v_all[:, :, DK:DK + 1], 1.0).then_inc(m["krow_in"], 1)
            gp.memset(qs[:, :, :].bitcast(F32), 0.0).then_inc(m["ones_in"], 1)
            link(gp.memset(pad_row[:, :], 0.0))
            link(gp.memset(pad_row[:, D + 2:D + 3], float(P)))
            gp.iota(pad_row[:, D:D + 1], pattern=[[0, 1]], base=TOPK * TOKENS, channel_multiplier=1,
                    allow_small_or_imprecise_dtypes=True).then_inc(m["const_in"], 1)
            gp.memset(ones_b[:, :], 1.0)
            gp.affine_select(out=before[:, :], in_=ones_f[:, :], compare_op=ALU.is_gt, fill=0.0, base=0,
                             pattern=[[1, P]], channel_multiplier=-1)
            gp.iota(rev8[:, :], pattern=[[-1, E]], base=E, channel_multiplier=0, allow_small_or_imprecise_dtypes=True)
            gp.iota(steps128[:, :], pattern=[[P, TILES]], base=0, channel_multiplier=0,
                    allow_small_or_imprecise_dtypes=True)
            gp.iota(tile_no[:, :], pattern=[[1, SORTED]], base=0, channel_multiplier=0,
                    allow_small_or_imprecise_dtypes=True)
            gp.iota(meta[:, :, :, 0], pattern=[[TOPK * P, TILES], [1, TOPK]], base=0, channel_multiplier=TOPK,
                    allow_small_or_imprecise_dtypes=True)
            gp.memset(row_st[:, :, :, :], 0.0)
            gp.memset(eid_f[:, :], 0.0)
            for i in range(8):
                gp.memset(pow8[:, i:i + 1], float(8 ** i))
            gp.memset(scan[:, :, :], 0.0).then_inc(m["const_in"], 1)

            def split_q(g, n):
                r = n % 2
                qv = q_all[:, bass.ds(g * 512, 512)]
                await_ge(pool, m["q_sb"], g + 1, m["pool_passed"])
                if n >= 2:
                    await_ge(pool, q_w[r], 32 * ((g - r) // 2), m["pool_passed"])
                gp.tensor_copy(q_parts[:, r, 0, :], qv).then_inc(m["qpart"], 1)
                await_ge(pool, m["qpart"], 4 * g + 1, m["pool_passed"])
                gp.tensor_tensor(q_rest[:, r, :], qv, q_parts[:, r, 0, :], ALU.subtract).then_inc(m["qpart"], 1)
                await_ge(pool, m["qpart"], 4 * g + 2, m["pool_passed"])
                gp.tensor_copy(q_parts[:, r, 1, :], q_rest[:, r, :]).then_inc(m["qpart"], 1)
                await_ge(pool, m["qpart"], 4 * g + 3, m["pool_passed"])
                gp.tensor_tensor(q_parts[:, r, 2, :], q_rest[:, r, :], q_parts[:, r, 1, :],
                                 ALU.subtract).then_inc(m["qpart"], 1)
                await_ge(pool, m["qpart"], 4 * g + 4, m["pool_passed"])
                for b in range(2):
                    gp.dma_start(q_dram[bass.ds(2 * g + b, 1)].rearrange("a i p s -> p (a i) s"),
                                 q_parts[:, r, :, b * S:(b + 1) * S]).then_inc(q_w[r], 16)

            PER = 6

            def scatter(t, n):
                r = n % 2
                done = PER * t
                if n >= 2:
                    await_ge(pool, scat[r], 32 * ((t - r) // 2), m["pool_passed"])
                gp.tensor_copy(r_col[:, r, :], lnb[:, 1, bass.ds(t, 1)]).then_inc(m["pool_row"], 1)
                gp.tensor_tensor(t_raw[:, r, :], xn_all[:, bass.ds(t, 1), :].rearrange("p a d -> p (a d)"),
                                 ns_row[:, :], ALU.mult).then_inc(m["pool_row"], 1)
                gp.tensor_copy(pos_st[:, r, :], pos_i[:, bass.ds(t, 1), :].rearrange("p a k -> p (a k)")
                               ).then_inc(m["pool_row"], 1)
                gp.tensor_copy(row_st[:, r, :, D:D + 2], meta[:, bass.ds(t, 1), :, :].rearrange("p a k c -> p (a k) c")
                               ).then_inc(m["pool_row"], 1)
                await_ge(pool, m["pool_row"], done + 4, m["pool_passed"])
                for k in range(TOPK):
                    gp.tensor_scalar(row_st[:, r, k, 0:D], t_raw[:, r, :], r_col[:, r, :], 1.0,
                                     ALU.mult, ALU.mult).then_inc(m["pool_row"], 1)
                await_ge(pool, m["pool_row"], done + PER, m["pool_passed"])
                for k in range(TOPK):
                    gp.indirect_dma_start(out=sorted_dram, out_offset=bass.IndirectOffsetOnAxis(ap=pos_st[:, r, k:k + 1], axis=0),
                                          in_=row_st[:, r, k, :], in_offset=None).then_inc(scat[r], 16)

            split_q(0, 0)
            split_q(1, 1)
            with pool.Fori(1, GROUPS // 2) as it:
                for h in range(2):
                    split_q(2 * it + h, 2 + h)
            await_ge(pool, m["route_ok"], 1, m["pool_passed"])
            await_ge(pool, m["pad_in"], 64, m["pool_passed"])
            await_ge(pool, m["w_in"], 16 * N_W, m["pool_passed"])
            for t in range(4):
                scatter(t, t)
            with pool.Fori(1, GROUPS - 1) as it:
                for r in range(4):
                    scatter(4 * it + r, 4 + r)
            for t in range(TILES - 4, TILES):
                scatter(t, t)

            def prepare(q, n):
                r = n % 4
                await_ge(pool, xs_in[r], 16 * ((q - r) // 4) + 16, m["pool_passed"])
                if n >= 4:
                    await_ge(pool, y_out[r], 32 * ((q - r) // 4), m["pool_passed"])
                gp.tensor_tensor(pad_at[:, r, :], xs[:, r, :, D + 2], tile_no[:, bass.ds(2 * q, 2)], ALU.mult
                                 ).then_inc(m["dest_ok"], 1)
                await_ge(pool, m["dest_ok"], 3 * q + 1, m["pool_passed"])
                gp.tensor_tensor(pad_at[:, r, :], xs[:, r, :, D], pad_at[:, r, :], ALU.add).then_inc(m["dest_ok"], 1)
                await_ge(pool, m["dest_ok"], 3 * q + 2, m["pool_passed"])
                if n >= 4:
                    await_ge(pool, m["y_ok"], 2 * (q - 3), m["pool_passed"])
                gp.tensor_copy(p_st[:, r, :], xs[:, r, :, D + 1]).then_inc(m["p_ok"], 1)
                gp.tensor_copy(dest_i[:, r, :], pad_at[:, r, :]).then_inc(m["dest_ok"], 1)
                await_ge(pool, m["dest_ok"], 3 * q + 3, m["pool_passed"])

            def send(q, n):
                r = n % 4
                await_ge(pool, m["y_ok"], 2 * q + 2, m["pool_passed"])
                for t in range(2):
                    gp.indirect_dma_start(out=y_dram, out_offset=bass.IndirectOffsetOnAxis(ap=dest_i[:, r, t:t + 1], axis=0),
                                          in_=ys[:, r, t, :], in_offset=None).then_inc(y_out[r], 16)

            for q in range(2):
                prepare(q, q)
            for q in range(2):
                send(q, q)
                prepare(q + 2, q + 2)
            with pool.Fori(1, PAIRS // 4) as it:
                for r in range(4):
                    send(4 * it + r - 2, 2 + r)
                    prepare(4 * it + r, 4 + r)
            for q in range(PAIRS - 2, PAIRS):
                send(q, q)

            for g in range(GROUPS):
                if on_pool(g + 2):
                    pool.wait_ge(yb_in[(g + 2) % 4], 16 * ((g + 2) // 4) + 16)
                    if g >= 2:
                        pool.wait_ge(m["o_ok"], g - 1)
                    gp.tensor_tensor(f_of(g + 2), xn_all[:, 4 * g + 8:4 * g + 12, :], yb[:, (g + 2) % 4, :, 0:D], ALU.add
                                     ).then_inc(m["fp_ok"], 1)
                await_ge(pool, m["so_ok"], g + 1, m["pool_passed"])
                gp.tensor_tensor(x_all[:, 4 * g:4 * g + 4, :], x_all[:, 4 * g:4 * g + 4, :], f_of(g), ALU.add
                                 ).then_inc(m["o_ok"], 1)

        @block.scalar
        def _(act):
            sc = nc.scalar
            projections = (
                (ns_col[:, :], nscale.rearrange("(d a) -> d a", a=1)),
                (w24_sb[:, :], w24), (wq_sb[:, :], wq),
                (sc_col[:, :], scale.rearrange("(a d) -> a d", a=1).to_broadcast([P, 1])),
            )
            for dst, src in projections:
                act.dma_start(dst, src).then_inc(m["wp_in"], 16)

            def deviation(h):
                act.wait_ge(m["var_ok"], h + 1)
                sc.activation(lnb[:, 3, QT * h:QT * h + QT], lnb[:, 2, QT * h:QT * h + QT], ACT.Sqrt
                              ).then_inc(m["std_ok"], 1)

            def evac_xT(g):
                act.wait_ge(m["xT_ps"], g + 1)
                if g >= 2:
                    act.wait_ge(m["kv_ps"], g - 1)
                sc.activation(xnT[:, g % 2, :], ps[:, g % 2, :], ACT.Copy).then_inc(m["xT_sb"], 1)

            def evac_q(g):
                act.wait_ge(m["q_ps"], g + 1)
                sc.activation(q_all[:, g * 512:(g + 1) * 512], ps[:, 2 + g % 2, :], ACT.Identity,
                              scale=sc_col[:, 0:1]).then_inc(m["q_sb"], 1)

            def evac_kv(g):
                act.wait_ge(m["kv_ps"], g + 1)
                sc.activation(kvg[:, 4 * g:4 * g + 4, :], ps[:, 4 + g % 2, 0:96].rearrange("p (t c) -> p t c", t=4),
                              ACT.Copy).then_inc(m["kv_sb"], 1)

            def evac_kst(i):
                act.wait_ge(m["kst_ps"], i + 1)
                sc.activation(k_stack[:, i * 1024:(i + 1) * 1024], key_bank[i].bitcast(BF16),
                              ACT.Copy).then_inc(m["kst_sb"], 1)

            act.wait_ge(m["prow"], 1)
            sc.activation(root1[:, :], ones_f[:, 0:1], ACT.Sqrt)
            deviation(0)
            for g in range(GROUPS + 1):
                if g < GROUPS:
                    evac_xT(g)
                if g == 1:
                    act.wait_ge(m["wp_in"], 16 * N_WP)
                if g >= 1:
                    evac_q(g - 1)
                    evac_kv(g - 1)
                if g < 3:
                    deviation(g + 1)
                if g == 6:
                    evac_kst(0)
                    evac_kst(1)
            def evac_roots():
                act.wait_ge(m["ms_ok"], 1)
                sc.activation(lnb[:, 5, :], lnb[:, 4, :], ACT.Sqrt).then_inc(m["rms_ok"], 1)

            def choice_exp():
                act.wait_ge(m["e_ok"], 1)
                sc.activation(rs[:, 5, :], rs[:, 4, :], ACT.Exp).then_inc(m["e_exp"], 1)

            def step(u, n):
                if 0 <= n < UNITS:
                    between(u, n)
                    for k in range(CH):
                        act.wait_ge(m["exp_ps"], CH * u + k + 1)
                        if k == 0 and n >= 2:
                            act.wait_ge(m["pv_ok"], u - 1)
                        sc.activation(probs[:, n % 2, k, :], ex_bank[BANKS[n % 2][k]], ACT.Exp).then_inc(m["exp_ok"], 1)
                        if k == EVAC_S_AT:
                            evac_s(u, n)
                        if k == EVAC_M_AT and n <= UNITS - 2:
                            evac_m(u, n)
                        if k == EVAC_ON_AT:
                            evac_on(u, n)
                else:
                    if n == -2:
                        evac_kst(2)
                        evac_kst(3)
                        evac_roots()
                    evac_s(u, n)
                    between(u, n)
                    if -1 <= n <= UNITS - 2:
                        evac_m(u, n)
                    if n == -1:
                        choice_exp()
                    evac_on(u, n)

            def between(u, n):
                if 0 <= n - 2 < UNITS:
                    act.wait_ge(m["pv_ok"], u - 1)
                    if n - 2 >= 2:
                        act.wait_ge(m["oT_ps"], u - 3)
                    sc.activation(o_T[:, n % 2, :], pv_bank, ACT.Copy).then_inc(m["oT_sb"], 1)

            def evac_m(u, n):
                act.wait_ge(m["mT_ps"], u + 2)
                if n + 1 >= 2:
                    act.wait_ge(m_in[(n + 1) % 2], 16 * ((u + 1 - (n + 1) % 2) // 2))
                sc.activation(m_T[:, (n + 1) % 2, :], mT_ps, ACT.Copy
                              ).then_inc(m["mT_sb"], 1)

            def evac_on(u, n):
                if n % 2 == 1 and 0 <= n - 3 < UNITS:
                    act.wait_ge(m["onT_ps"], (u - 1) // 2)
                    sc.activation(o_nT[:, :], onT_ps, ACT.Copy).then_inc(m["onT_sb"], 1)

            def evac_s(u, n):
                if n % 2 == 0 and 0 <= n - 4 < UNITS:
                    act.wait_ge(m["s_ps"], (u - 2) // 2)
                    if n == 4:
                        act.wait_ge(m["route_ok"], 1)
                    sc.activation(s_all[:, bass.ds(u - 4, 2), :], s_ps.rearrange("p (t d) -> p t d", t=2),
                                  ACT.Copy, scale=0.5).then_inc(m["s_ok"], 1)

            attention(act, step)

            def expert(q, n):
                if 0 <= n - 2 < PAIRS:
                    act.wait_ge(m["hT_ps"], q - 1)
                    if n - 2 >= 1:
                        act.wait_ge(m["y_ps"], q - 2)
                    sc.activation(hT, ps[:, 5, :], ACT.Copy, scale=0.5).then_inc(m["hT_sb"], 1)
                if 0 <= n + 1 < PAIRS:
                    act.wait_ge(m["xsT_ps"], q + 2)
                    if n == -1:
                        act.wait_ge(m["pv_ok"], UNITS - 1)
                    if n + 1 >= 2:
                        act.wait_ge(m["h_ps"], q)
                    sc.activation(xT[:, (n + 1) % 2, :], ps[:, 6, 0:256], ACT.Copy).then_inc(m["xsT_sb"], 1)
                if 0 <= n < PAIRS:
                    act.wait_ge(m["g_ok"], q + 1)
                    if n >= 2:
                        act.wait_ge(m["gt_ok"], q - 1)
                    sc.activation(th[:, n % 2, :], glu[:, n % 2, :], ACT.Tanh, scale=ALPHA / 2).then_inc(m["th_ok"], 1)
                if 0 <= n - 2 < PAIRS:
                    act.wait_ge(m["y_ps"], q - 1)
                    act.wait_ge(m["p_ok"], q - 1)
                    if n - 2 >= 4:
                        act.wait_ge(y_out[(n - 2) % 4], 32 * ((q - 2 - (n - 2) % 4) // 4))
                    for t in range(2):
                        sc.activation(ys[:, (n - 2) % 4, t, :], ps[:, 4, t * D:(t + 1) * D], ACT.Identity,
                                      scale=p_st[:, (n - 2) % 4, t:t + 1]).then_inc(m["y_ok"], 1)

            last_and_first(step, expert)
            experts(act, expert)

            for g in range(GROUPS):
                act.wait_ge(m["f_ok"], g + 1)
                sc.activation(fb[:, 4 + g % 4, :, :], f_of(g), ACT.Tanh, scale=0.5).then_inc(m["fth_ok"], 1)

        @block.tensor
        def _(pe):
            te = nc.tensor
            pe.wait_ge(m["ident_ok"], 1)

            def turn_keys(i):
                pe.wait_ge(m["krow_ok"], i // 2 + 1)
                for t in range(8):
                    last = te.transpose(key_bank[i].bitcast(BF16)[:, t * P:(t + 1) * P],
                                        k_rows[:, 8 * i + t, :], ident_b[:, :])
                last.then_inc(m["kst_ps"], 1)

            for g in range(GROUPS + 1):
                if g < GROUPS:
                    pe.wait_ge(m["xn_ok"], 4 * g + 4)
                    if g >= 2:
                        pe.wait_ge(m["xT_sb"], g - 1)
                    for t in range(4):
                        last = te.transpose(ps[:, g % 2, t * P:(t + 1) * P], xn_all[:, 4 * g + t, :], ident[:, :])
                    last.then_inc(m["xT_ps"], 1)
                if g >= 1:
                    r = (g - 1) % 2
                    pe.wait_ge(m["xT_sb"], g)
                    if g == 1:
                        pe.wait_ge(m["wp_in"], 16 * N_WP)
                        pe.wait_ge(m["w24_ok"], 1)
                    if g >= 3:
                        pe.wait_ge(m["q_sb"], g - 2)
                        pe.wait_ge(m["kv_sb"], g - 2)
                    te.matmul(ps[:, 2 + r, :], wq_sb[:, :], xnT[:, r, :], start=True, stop=True).then_inc(m["q_ps"], 1)
                    for t in range(4):
                        last = te.matmul(ps[:, 4 + r, t * 24:(t + 1) * 24], xnT[:, r, t * P:(t + 1) * P],
                                         w24_sb[:, :], start=True, stop=True)
                    last.then_inc(m["kv_ps"], 1)
                if g == 6:
                    turn_keys(0)
                    turn_keys(1)
            pe.wait_ge(m["const_in"], 2)
            pe.wait_ge(m["w_in"], 16 * N_W)
            pe.wait_ge(m["kv_sb"], GROUPS)
            pe.wait_ge(m["kst_sb"], 2)
            pe.wait_ge(m["q_sb"], GROUPS)
            pe.wait_ge(m["xT_sb"], GROUPS)

            def chunks_since(n, k):
                return 1 + (BANKS[1 - n % 2] + BANKS[n % 2][:k])[::-1].index(BANKS[n % 2][k])

            def scores_exp(u, n, k):
                tt, j = k // 4, k % 4
                if k == 0:
                    pe.wait_ge(m_in[n % 2], 16 * ((u - n % 2) // 2) + 16)
                    pe.wait_ge(ke_in[(n // 2) % 2], 16 * ((u - n % 4) // 4) + 16)
                bank, since = BANKS[n % 2][k], chunks_since(n, k)
                if n > 0 or k >= since:
                    pe.wait_ge(m["exp_ok"], CH * u + k - since + 1)
                te.matmul(ex_bank[bank], k_exp[:, (n // 2) % 2, tt * P:(tt + 1) * P],
                          qs[:, n % 4, j * 512:(j + 1) * 512], start=True, stop=True).then_inc(m["exp_ps"], 1)

            def scores_max(u, n, k):
                st, j = k // 4, k % 4
                if k == 0:
                    pe.wait_ge(qs_in[n % 4], 16 * ((u - n % 4) // 4) + 16)
                    pe.wait_ge(km_in[(n // 2) % 2], 16 * ((u - n % 4) // 4) + 16)
                bank, since = BANKS[n % 2][k], chunks_since(n, k)
                if n > 0 or k >= since:
                    pe.wait_ge(m["max_ok"], CH * u + k - since + 1)
                for e in range(2):
                    at = (2 * j + e) * S + st * P
                    last = te.matmul(mx_bank[bank][:, e * S:(e + 1) * S], qs[0:MROW, n % 4, at:at + P],
                                     k_max[0:MROW, (n // 2) % 2, :], start=True, stop=True)
                last.then_inc(m["max_ps"], 1)

            def values(v, n, tt):
                if tt == 0:
                    pe.wait_ge(m["exp_ok"], CH * v + CH)
                    pe.wait_ge(v_in[(n // 2) % 2], 16 * ((v - n % 4) // 4) + 16)
                    if n >= 1:
                        pe.wait_ge(m["on_ok"], 2 * v)
                    if n == 0:
                        pe.wait_ge(m["kst_sb"], 4)
                        pe.wait_ge(m["rank_sb"], 1)
                for j in range(4):
                    last = te.matmul(pv_bank[32 * j:32 * j + 32, :], v_use[:, (n // 2) % 2, tt, :],
                                     probs[:, n % 2, 4 * tt + j, :], start=(tt == 0), stop=(tt == 1))
                if tt == 1:
                    last.then_inc(m["pv_ok"], 1)

            def turn_m(u, n):
                if not -1 <= n <= UNITS - 2:
                    return
                pe.wait_ge(m["mpart"], 5 * (u + 2))
                if n % 2 == 0 and n >= 4:
                    pe.wait_ge(m["s_ok"], (u - 2) // 2)
                elif n >= 0:
                    pe.wait_ge(m["mT_sb"], u + 1)
                for st in range(2):
                    last = te.transpose(mT_ps[:, st * P:(st + 1) * P],
                                        m_parts[:, (n + 1) % 2, st, :, :].rearrange("p i h -> p (i h)"), ident_b[:, :])
                last.then_inc(m["mT_ps"], 1)

            def ranks():
                pe.wait_ge(m["oh_ok"], 1)
                te.matmul(pv_bank[:, 0:256], before[:, :], oh_b[:, :], start=True, stop=True)
                te.matmul(pv_bank[:, 256:512], ones_b[:, :], oh_b[:, :], start=True, stop=True
                          ).then_inc(m["rank_ps"], 1)

            def turn_o(u, n):
                if 0 <= n - 2 < UNITS:
                    pe.wait_ge(m["oT_sb"], u - 1)
                    for i in range(4):
                        last = te.transpose(pv_bank[:, i * P:(i + 1) * P], o_T[:, n % 2, i * P:(i + 1) * P], ident[:, :])
                    last.then_inc(m["oT_ps"], 1)

            def turn_on(u, n):
                if n % 2 == 1 and 0 <= n - 3 < UNITS:
                    pe.wait_ge(m["on_ok"], 2 * (u - 1))
                    pe.wait_ge(m["mT_sb"], (u + 2) if n <= UNITS - 2 else UNITS)
                    for st in range(2):
                        last = te.transpose(onT_ps[:, st * P:(st + 1) * P], o_n[:, st, :], ident[:, :])
                    last.then_inc(m["onT_ps"], 1)

            def project(u, n):
                if n % 2 == 0 and 0 <= n - 4 < UNITS:
                    pe.wait_ge(m["onT_sb"], (u - 2) // 2)
                    for st in range(2):
                        last = te.matmul(s_ps[:, st * D:(st + 1) * D], o_nT[:, st * P:(st + 1) * P], wout_sb[:, :],
                                         start=True, stop=True)
                    last.then_inc(m["s_ps"], 1)

            def step(u, n):
                for k in range(CH):
                    if 0 <= n < UNITS:
                        scores_exp(u, n, k)
                    if n + 2 < UNITS:
                        scores_max(u + 2, n + 2, k)
                    if n == -2 and k == 4:
                        turn_keys(2)
                        turn_keys(3)
                    if k == PROJECT_AT:
                        project(u, n)
                    if k == TURN_O_AT:
                        turn_o(u, n)
                    if k == 2 and n == 1:
                        ranks()
                    if k == TURN_M_AT:
                        turn_m(u, n)
                    if k == TURN_ON_AT:
                        turn_on(u, n)
                    if k in VALUES_AT and 0 <= n - 1 < UNITS:
                        values(u - 1, n - 1, VALUES_AT.index(k))

            attention(pe, step)

            packed = [None, None]

            def expert(q, n):
                if n == -1:
                    pe.wait_ge(m["max_ok"], CH * UNITS)
                if n == 0:
                    pe.wait_ge(m["exp_ok"], CH * UNITS)
                    pe.wait_ge(m["bias_r"], 16)
                    pe.wait_ge(m["w1_in"], 64)
                    pe.wait_ge(m["w2_in"], 16)
                if n == 2:
                    pe.wait_ge(m["on_ok"], 2 * UNITS)
                if n >= 0 and n % 4 == 0:
                    for h in range(2):
                        if h == 1 or n < PAIRS:
                            packed[h] = pe.value_load(eid_i[0:1, h, bass.ds((q - n % 4) // 4, 1)],
                                                      min_val=0, max_val=8 ** 8 - 1)
                if 0 <= n - 2 < PAIRS:
                    r = n % 2
                    pe.wait_ge(m["hid_ok"], q - 1)
                    if n - 2 >= 1:
                        pe.wait_ge(m["hT_sb"], q - 2)
                    for i in range(4):
                        last = te.transpose(ps[:, 5, i * P:(i + 1) * P], hid[:, r, i * P:(i + 1) * P], ident[:, :])
                    last.then_inc(m["hT_ps"], 1)
                if 0 <= n + 1 < PAIRS:
                    pe.wait_ge(xs_in[(n + 1) % 4], 16 * ((q + 1 - (n + 1) % 4) // 4) + 16)
                    if n + 1 >= 1:
                        pe.wait_ge(m["xsT_sb"], q + 1)
                    for t in range(2):
                        last = te.transpose(ps[:, 6, t * P:(t + 1) * P], xs[:, (n + 1) % 4, t, 0:D], ident[:, :])
                    last.then_inc(m["xsT_ps"], 1)
                if 0 <= n < PAIRS:
                    if n >= 2:
                        pe.wait_ge(m["l_ok"], q - 1)
                    await_ge(pe, m["xsT_sb"], q + 1, m["pe_passed"])
                    for t in range(2):
                        e = pe.snap((packed[0] >> (3 * (2 * (n % 4) + t))) & (E - 1))
                        bank = ps[:, 2 * (n % 2) + t, :]
                        te.matmul(bank, ones_b[0:3, :], bias_rows[:, bass.ds(e * 2 * INNER, 2 * INNER)], start=True, stop=False)
                        last = te.matmul(bank, xT[:, n % 2, t * P:(t + 1) * P], w1_sb[:, bass.ds(e * 2 * INNER, 2 * INNER)],
                                         start=False, stop=True)
                    last.then_inc(m["h_ps"], 1)
                if 0 <= n - 2 < PAIRS:
                    if n - 2 >= 1:
                        pe.wait_ge(m["y_ok"], 2 * (q - 2))
                    await_ge(pe, m["hT_sb"], q - 1, m["pe_passed"])
                    for t in range(2):
                        e = pe.snap((packed[1] >> (3 * (2 * (n % 4) + t))) & (E - 1))
                        yt = ps[:, 4, t * D:(t + 1) * D]
                        te.matmul(yt, ones_b[0:3, :], bias_rows[:, bass.ds(e * D + E * 2 * INNER, D)], start=True, stop=False)
                        for c in range(2):
                            last = te.matmul(yt, hT[:, (2 * t + c) * P:(2 * t + c + 1) * P],
                                             w2_sb[:, bass.ds(e * 2 * D + c * D, D)], start=False, stop=(c == 1))
                    last.then_inc(m["y_ps"], 1)

            last_and_first(step, expert)
            experts(pe, expert)

        @block.vector
        def _(dve):
            ve = nc.vector
            count = [0]

            def link(ins):
                count[0] += 1
                ins.then_inc(m["dve"], 1)
                dve.wait_ge(m["dve"], count[0])

            def statistics(h):
                dve.wait_ge(x_in[h], 16)
                for t in range(QT * h, QT * h + QT):
                    last = ve.bn_stats(st6[:, t, :], x_all[:, t, :])
                last.then_inc(m["stat"], 1)
                dve.wait_ge(m["stat"], 2 * h + 1)
                for t in range(QT * h, QT * h + QT):
                    last = ve.bn_aggr(mv[:, t, :], st6[:, t, :])
                last.then_inc(m["stat"], 1)
                dve.wait_ge(m["stat"], 2 * h + 2)
                ve.tensor_scalar(lnb[:, 2, QT * h:QT * h + QT], mv[:, QT * h:QT * h + QT, 1], EPS, None, ALU.add
                                 ).then_inc(m["var_ok"], 1)

            def norm(h):
                dve.wait_ge(m["std_ok"], h + 1)
                link(ve.reciprocal(lnb[:, 0, QT * h:QT * h + QT], lnb[:, 3, QT * h:QT * h + QT]))
                for t in range(QT * h, QT * h + QT):
                    ve.tensor_scalar(xn_all[:, t, :], x_all[:, t, :], mv[:, t, 0:1], lnb[:, 0, t:t + 1],
                                     ALU.subtract, ALU.mult).then_inc(m["xn_ok"], 1)

            def key_rows(h):
                a, b = 16 * h, 16 * h + 16
                dve.wait_ge(m["kv_sb"], 4 * h + 4)
                kf = kvg[:, a:b, E:E + DK]
                link(ve.tensor_copy(k_p[:, 0, a:b, :], kf))
                link(ve.tensor_tensor(k_rest[:, 0, a:b, :], kf, k_p[:, 0, a:b, :], ALU.subtract))
                link(ve.tensor_copy(k_p[:, 1, a:b, :], k_rest[:, 0, a:b, :]))
                link(ve.tensor_tensor(k_p[:, 2, a:b, :], k_rest[:, 0, a:b, :], k_p[:, 1, a:b, :], ALU.subtract))
                for jj in range(3):
                    at = 3 * jj * DK
                    last = ve.tensor_copy(k_rows[:, a:b, at:at + 3 * DK].rearrange("p t (i d) -> p t i d", i=3),
                                          replicated(k_p[:, jj, a:b, :], 3, 2))
                last.then_inc(m["krow_ok"], 1)
                ve.tensor_copy(v_all[:, a:b, 0:DK], kvg[:, a:b, E + DK:24]).then_inc(m["v_ok"], 1)

            statistics(0)
            norm(0)
            statistics(1)
            dve.wait_ge(m["wp_in"], 16 * N_WP)
            ve.tensor_scalar(w24_sb[:, 0:E], w24_sb[:, 0:E], ns_col[:, 0:1], None, ALU.mult).then_inc(m["w24_ok"], 1)
            norm(1)
            statistics(2)
            statistics(3)
            norm(2)
            norm(3)
            dve.wait_ge(m["krow_in"], 2)
            key_rows(0)
            def second_half():
                key_rows(1)
                link(ve.tensor_tensor(lnb[:, 6, :], mv[:, :, 1], rstd, ALU.mult))
                link(ve.tensor_tensor(lnb[:, 7, :], lnb[:, 6, :], rstd, ALU.mult))
                ve.tensor_scalar(lnb[:, 4, :], lnb[:, 7, :], EPS, None, ALU.add).then_inc(m["ms_ok"], 1)
                dve.wait_ge(m["w_in"], 16 * N_W)
                link(ve.tensor_copy(bias_parts[:, 0, :], bias_in[:, :]))
                link(ve.tensor_tensor(bias_rest[:, 0, :], bias_in[:, :], bias_parts[:, 0, :], ALU.subtract))
                link(ve.tensor_copy(bias_parts[:, 1, :], bias_rest[:, 0, :]))
                ve.tensor_tensor(bias_parts[:, 2, :], bias_rest[:, 0, :], bias_parts[:, 1, :], ALU.subtract).then_inc(m["bias_ok"], 1)

            def t3(i):
                return rt[:, i, :].rearrange("p (t e) -> p t e", e=E)

            def over_e(col):
                return replicated(col, E, 2)

            def over_t(row):
                return replicated(row, TILES, 1)

            def mark(ins):
                count[0] += 1
                ins.then_inc(m["dve"], 1)

            def best_two():
                dve.wait_ge(m["const_in"], 2)
                dve.wait_ge(m["rms_ok"], 1)
                mark(ve.reciprocal(rms, lnb[:, 5, :]))
                yield
                mark(ve.tensor_tensor(t3(0), kvg[:, :, 0:E], over_e(rms), ALU.mult))
                yield
                mark(ve.tensor_tensor(t3(1), t3(0), over_t(gb_row[:, :]), ALU.add))
                yield
                mark(ve.tensor_reduce(rs[:, 0, :], t3(1), AX, ALU.max))
                yield
                mark(ve.tensor_tensor(t3(2), t3(1), over_e(rs[:, 0, :]), ALU.is_equal))
                yield
                mark(ve.tensor_tensor(t3(3), t3(2), over_t(rev8[:, :]), ALU.mult))
                yield
                mark(ve.tensor_reduce(rs[:, 1, :], t3(3), AX, ALU.max))
                yield
                mark(ve.tensor_tensor(t3(4), t3(3), over_e(rs[:, 1, :]), ALU.is_equal))
                yield
                mark(ve.scalar_tensor_tensor(t3(5), t3(4), -BIG, t3(1), ALU.mult, ALU.add))
                yield
                mark(ve.tensor_reduce(rs[:, 2, :], t3(5), AX, ALU.max))
                yield
                ve.tensor_tensor(rs[:, 4, :], rs[:, 2, :], rs[:, 0, :], ALU.subtract).then_inc(m["e_ok"], 1)
                mark(ve.tensor_tensor(t3(6), t3(5), over_e(rs[:, 2, :]), ALU.is_equal))
                yield
                mark(ve.tensor_tensor(t3(7), t3(6), over_t(rev8[:, :]), ALU.mult))
                yield
                mark(ve.tensor_reduce(rs[:, 3, :], t3(7), AX, ALU.max))
                yield
                mark(ve.tensor_tensor(t3(8), t3(7), over_e(rs[:, 3, :]), ALU.is_equal))
                yield
                ve.tensor_tensor(oh_b[:, :], rt[:, 4, :], rt[:, 8, :], ALU.add).then_inc(m["oh_ok"], 1)
                dve.wait_ge(m["e_exp"], 1)
                mark(ve.tensor_scalar(rs[:, 6, :], rs[:, 5, :], 1.0, None, ALU.add))
                yield
                mark(ve.reciprocal(rs[:, 7, :], rs[:, 6, :]))
                yield
                ve.tensor_copy(meta[:, :, 0, 1], rs[:, 7, :])
                ve.tensor_tensor(meta[:, :, 1, 1], rs[:, 7, :], rs[:, 5, :], ALU.mult)

            def sorted_places():
                pad = 16 * E
                tot = t3(0)
                rank = t3(1)
                dve.wait_ge(m["rank_ps"], 1)
                ve.tensor_copy(rt[:, 1, :], pv_bank[:, 0:256])
                ve.tensor_copy(rt[:, 0, :], pv_bank[:, 256:512]).then_inc(m["rank_sb"], 1)
                dve.wait_ge(m["rank_sb"], 1)
                mark(ve.tensor_copy(scan[:, 0, pad:], tot.rearrange("p t e -> p (t e)")))
                yield
                src = 0
                for d in (1, 2, 4, 8, 16):
                    mark(ve.tensor_tensor(scan[:, 1 - src, pad:], scan[:, src, pad:],
                                          scan[:, src, pad - d * E:pad - d * E + TILES * E], ALU.add))
                    yield
                    src = 1 - src
                incl = scan[:, src, pad:].rearrange("p (t e) -> p t e", e=E)
                counts = scan[:, src, pad + (TILES - 1) * E:]
                mark(ve.tensor_tensor(t3(9), incl, tot, ALU.subtract))
                yield
                mark(ve.tensor_tensor(t3(10), t3(9), rank, ALU.add))
                yield
                mark(ve.memset(nt[:, :, :], 0.0))
                yield
                mark(ve.tensor_tensor(cmp_n[:, :, :], replicated(counts, TILES, 2), replicated(steps128[:, :], E, 1), ALU.is_gt))
                yield
                mark(ve.tensor_reduce(nt[:, 0, 8:16], cmp_n[:, :, :], AX, ALU.add))
                yield
                for i, d in enumerate((1, 2, 4)):
                    mark(ve.tensor_tensor(nt[:, i + 1, 8:16], nt[:, i, 8:16], nt[:, i, 8 - d:16 - d], ALU.add))
                    yield
                mark(ve.tensor_tensor(nt[:, 4, 8:16], nt[:, 3, 8:16], nt[:, 0, 8:16], ALU.subtract))
                yield
                mark(ve.tensor_scalar(nt[:, 5, 8:16], nt[:, 4, 8:16], float(P), None, ALU.mult))
                yield
                mark(ve.tensor_tensor(t3(11), t3(10), over_t(nt[:, 5, 8:16]), ALU.add))
                yield
                for k, oh in enumerate((4, 8)):
                    mark(ve.tensor_tensor(t3(9), t3(oh), t3(11), ALU.mult))
                    yield
                    mark(ve.tensor_reduce(rs[:, 8 + k, :], t3(9), AX, ALU.add))
                    yield
                    ve.tensor_copy(pos_i[:, :, k], rs[:, 8 + k, :])
                mark(ve.tensor_tensor(cmp_t[:, :, :], replicated(tile_no[:, :], E, 2),
                                      replicated(nt[:, 3, 8:16], SORTED, 1), ALU.is_ge))
                yield
                mark(ve.tensor_reduce(cmp_s[:, :], cmp_t[:, :, :], AX, ALU.add))
                yield
                mark(ve.tensor_scalar(eid_f[:, 4:4 + SORTED], cmp_s[:, :], float(E - 1), None, ALU.min))
                yield
                for h, at in enumerate((4, 0)):
                    tiles8 = eid_f[:, at:at + 80].rearrange("p (i j) -> p i j", j=8)
                    mark(ve.tensor_tensor(eid_p[:, :, :], tiles8, replicated(pow8[:, :], 10, 1), ALU.mult))
                    yield
                    mark(ve.tensor_reduce(eid_s[:, h, :], eid_p[:, :, :], AX, ALU.add))
                    yield
                ve.tensor_copy(eid_i[:, :, :], eid_s[0:1, :, :]).then_inc(m["route_ok"], 1)

            routing = [best_two(), sorted_places()]

            def advance(part):
                dve.wait_ge(m["dve"], count[0])
                return next(part, True)

            def route(n, k):
                if n < 1:
                    advance(routing[0])
                elif n > 1 or k >= 4:
                    advance(routing[1])

            def normalise(u, n, stage):
                if not 0 <= n - 2 < UNITS:
                    return
                c = n % 2
                ov = pv_bank.rearrange("p (e t j d) -> p e t j d", e=2, t=2, j=4)
                if stage == 0:
                    dve.wait_ge(m["oT_ps"], u - 1)
                    if n >= 3:
                        dve.wait_ge(m["on_ok"], 2 * (u - 2))
                    ve.reciprocal(inv_sum[:, c, :, :], pv_bank.rearrange("p (i j d) -> p i j d", i=4, j=4)[:, :, :, DK]
                                  ).then_inc(m["inv_ok"], 1)
                    return
                dve.wait_ge(m["inv_ok"], u - 1)
                if c == 0 and n >= 4:
                    dve.wait_ge(m["onT_ps"], (u - 2) // 2)
                for st in range(2):
                    dst = o_n[:, st, :].rearrange("p (c j e d) -> p c e j d", c=2, j=4, e=2)[:, c, :, :, :]
                    inv = inv_sum[:, c, :, :].rearrange("p (e t) j -> p e t j", e=2)[:, :, st, :]
                    ve.tensor_tensor(dst, ov[:, :, st, :, 0:DK], replicated(inv, DK, 3), ALU.mult
                                     ).then_inc(m["on_ok"], 1)

            def split_m(u, n, stage):
                r = n % 2
                mx = maxes[:, r, :, :]
                if stage == 0:
                    dve.wait_ge(m["max_ok"], CH * u + CH)
                    if n >= 2:
                        dve.wait_ge(m["mT_ps"], u - 1)
                    ve.tensor_scalar(m_parts[:, r, :, 0, :], mx, -1.0, None, ALU.mult).then_inc(m["mpart"], 1)
                elif stage == 1:
                    dve.wait_ge(m["mpart"], 5 * u + 1)
                    ve.tensor_tensor(m_rest[:, r, 0, :, :], mx, m_parts[:, r, :, 0, :], ALU.add).then_inc(m["mpart"], 1)
                    dve.wait_ge(m["mpart"], 5 * u + 2)
                    ve.tensor_scalar(m_parts[:, r, :, 1, :], m_rest[:, r, 0, :, :], -1.0, None, ALU.mult
                                     ).then_inc(m["mpart"], 1)
                else:
                    dve.wait_ge(m["mpart"], 5 * u + 3)
                    ve.tensor_tensor(m_rest[:, r, 1, :, :], m_rest[:, r, 0, :, :], m_parts[:, r, :, 1, :], ALU.add
                                     ).then_inc(m["mpart"], 1)
                    dve.wait_ge(m["mpart"], 5 * u + 4)
                    ve.tensor_scalar(m_parts[:, r, :, 2, :], m_rest[:, r, 1, :, :], -1.0, None, ALU.mult
                                     ).then_inc(m["mpart"], 1)

            def step(u, n):
                if n + 2 < UNITS:
                    for k in range(CH):
                        st, j = k // 4, k % 4
                        dve.wait_ge(m["max_ps"], CH * (u + 2) + k + 1)
                        ve.tensor_reduce(maxes[:, n % 2, st, 2 * j:2 * j + 2],
                                         mx_bank[BANKS[n % 2][k]].rearrange("p (e t) -> p e t", e=2), AX, ALU.max
                                         ).then_inc(m["max_ok"], 1)
                        if n == -2 and k == HALF_AT:
                            second_half()
                        if n < 4 and (n > -2 or k > HALF_AT + 1):
                            route(n, k)
                        if k < 2 and n > -2:
                            split_m(u + 1, n + 1, k + 1)
                        if k in (NORM_AT, NORM_AT + 1):
                            normalise(u, n, k - NORM_AT)
                    split_m(u + 2, n + 2, 0)
                    if n == 3:
                        while not advance(routing[1]):
                            pass
                else:
                    if n == UNITS - 2:
                        split_m(u + 1, n + 1, 1)
                        split_m(u + 1, n + 1, 2)
                    normalise(u, n, 0)
                    normalise(u, n, 1)

            attention(dve, step)
            def expert(q, n):
                if not 0 <= n < PAIRS:
                    return
                r = n % 2
                hb = ps[:, 2 * r:2 * r + 2, :]
                g3 = glu[:, r, :].rearrange("p (t c) -> p t c", t=2)
                l3 = lin[:, r, :].rearrange("p (t c) -> p t c", t=2)
                dve.wait_ge(m["h_ps"], q + 1)
                if n == 0:
                    dve.wait_ge(m["pv_ok"], UNITS)
                if n >= 2:
                    dve.wait_ge(m["gt_ok"], q - 1)
                    dve.wait_ge(m["hid_ok"], q - 1)
                ve.tensor_scalar(g3, hb[:, :, 0:INNER], LIMIT, None, ALU.min).then_inc(m["g_ok"], 1)
                ve.tensor_scalar(l3, hb[:, :, INNER:], LIMIT, -LIMIT, ALU.min, ALU.max).then_inc(m["l_ok"], 1)
                dve.wait_ge(m["g_ok"], q + 1)
                dve.wait_ge(m["th_ok"], q + 1)
                ve.scalar_tensor_tensor(gt[:, r, :], th[:, r, :], 1.0, glu[:, r, :], ALU.add, ALU.mult).then_inc(m["gt_ok"], 1)
                dve.wait_ge(m["gt_ok"], q + 1)
                dve.wait_ge(m["l_ok"], q + 1)
                if n >= 2:
                    dve.wait_ge(m["hT_ps"], q - 1)
                ve.scalar_tensor_tensor(hid[:, r, :], lin[:, r, :], 1.0, gt[:, r, :], ALU.add, ALU.mult).then_inc(m["hid_ok"], 1)

            last_and_first(step, expert)
            experts(dve, expert)
            dve.wait_ge(m["s_ok"], B)

            def add_up(g, choice):
                f = f_of(g)
                if choice == 0 and on_pool(g):
                    dve.wait_ge(m["fp_ok"], g // 2)
                elif choice == 0:
                    dve.wait_ge(yb_in[g % 4], 16 * (g // 4) + 16)
                    if g >= 4:
                        dve.wait_ge(m["o_ok"], g - 3)
                    ve.tensor_tensor(f, xn_all[:, 4 * g:4 * g + 4, :], yb[:, g % 4, :, 0:D], ALU.add).then_inc(m["fy_ok"], 1)
                else:
                    if not on_pool(g):
                        dve.wait_ge(m["fy_ok"], sum(not on_pool(i) for i in range(g + 1)))
                    ve.tensor_tensor(f, f, yb[:, g % 4, :, D:2 * D], ALU.add).then_inc(m["f_ok"], 1)

            add_up(0, 0)
            add_up(0, 1)
            for g in range(GROUPS):
                f = f_of(g)
                if g + 1 < GROUPS:
                    add_up(g + 1, 0)
                dve.wait_ge(m["f_ok"], g + 1)
                dve.wait_ge(m["fth_ok"], g + 1)
                ve.scalar_tensor_tensor(f, fb[:, 4 + g % 4, :, :], 1.0, f, ALU.add, ALU.mult).then_inc(m["silu_ok"], 1)
                if g + 1 < GROUPS:
                    add_up(g + 1, 1)
                dve.wait_ge(m["silu_ok"], g + 1)
                ve.tensor_tensor(f, f, s_all[:, 4 * g:4 * g + 4, :], ALU.mult).then_inc(m["so_ok"], 1)

def kernel(L0_attn_x, L0_attn_w_q, L0_attn_w_k, L0_attn_w_v, L0_attn_w_out, L0_attn_softmax_scale,
           L0_ffn_norm_scale, L0_ffn_gate_w, L0_ffn_gate_b, L0_ffn_mlp1_w, L0_ffn_mlp1_b, L0_ffn_mlp2_w,
           L0_ffn_mlp2_b):
    import concourse.bacc as bacc
    from concourse.bass_utils import run_bass_kernel_spmd

    order = [4 * j + 2 * c + e for c in range(2) for j in range(4) for e in range(2)]
    a = {}
    a["x"] = np.ascontiguousarray(L0_attn_x).reshape(TOKENS, D)
    wq = np.asarray(L0_attn_w_q).reshape(HEADS, DK, D)[order]
    a["wq"] = np.ascontiguousarray(wq.transpose(2, 1, 0).reshape(D, D))
    a["w24"] = np.ascontiguousarray(np.concatenate(
        [np.asarray(L0_ffn_gate_w), np.asarray(L0_attn_w_k).T, np.asarray(L0_attn_w_v).T], axis=1))
    wo = np.asarray(L0_attn_w_out).reshape(D, HEADS, DK)[:, order]
    a["wout"] = np.ascontiguousarray(wo.reshape(D, D).T)
    a["nscale"] = np.ascontiguousarray(L0_ffn_norm_scale)
    a["gate_b"] = np.ascontiguousarray(L0_ffn_gate_b)
    w1 = np.asarray(L0_ffn_mlp1_w).reshape(E, D, INNER, 2)
    a["w1"] = np.ascontiguousarray(w1.transpose(1, 0, 3, 2).reshape(D, E * 2 * INNER))
    a["b1"] = np.ascontiguousarray(np.asarray(L0_ffn_mlp1_b).reshape(E, INNER, 2).transpose(0, 2, 1).reshape(-1))
    w2 = np.asarray(L0_ffn_mlp2_w).reshape(E, 2, P, D)
    a["w2"] = np.ascontiguousarray(w2.transpose(2, 0, 1, 3).reshape(P, E * 2 * D))
    a["b2"] = np.ascontiguousarray(L0_ffn_mlp2_b).reshape(-1)
    a["scale"] = np.ascontiguousarray(L0_attn_softmax_scale)

    nc = bacc.Bacc("TRN2", target_bir_lowering=False, num_devices=1)
    arrays = {f"in_{k}": v for k, v in a.items()}
    args = [nc.dram_tensor(k, v.shape, mybir.dt.from_np(v.dtype), kind="ExternalInput").ap() for k, v in arrays.items()]
    out = nc.dram_tensor("out_0", (TOKENS, D), F32, kind="ExternalOutput").ap()
    build(nc, *args, out)
    res = run_bass_kernel_spmd(nc, [arrays], core_ids=[0])
    return res.results[0]["out_0"].reshape(B, S, D)
```
